# Optimizing a Trainium2 kernel written in Bass

```python
import numpy as np
import jax
import jax.numpy as jnp

def _softmax(x, axis=-1):
    return jax.nn.softmax(x, axis=axis)

def _gelu(x):
    return jax.nn.gelu(x, approximate=True)

def _silu(x):
    return jax.nn.silu(x)

def _sigmoid(x):
    return jax.nn.sigmoid(x)

def _layernorm(x, axis=-1, eps=1e-05):
    m = jnp.mean(x, axis=axis, keepdims=True)
    v = jnp.var(x, axis=axis, keepdims=True)
    return (x - m) / jnp.sqrt(v + eps)

def _scatter_add(tgt, idx, src, axis=0):
    return tgt.at[idx].add(src)

def _segment_sum(src, seg, n):
    return jax.ops.segment_sum(src, seg, n)
kernel_name = 'mk_gps_d1_gnn_r8_9af66a'

def setup_inputs(seed: int=0):
    np.random.seed(seed)
    _w = jnp.asarray

    def _rec_inputs():
        import jax
        import jax.numpy as jnp
        _gk = jax.random.key(seed)
        x = -0.0002117 + 1 * jax.random.normal(jax.random.fold_in(_gk, 1), (12500, 256), jnp.float32)
        src = jax.random.randint(jax.random.fold_in(_gk, 2), (200000,), 0, 12500, jnp.int32)
        dst = jnp.minimum((12500 * jax.random.uniform(jax.random.fold_in(_gk, 3), (200000,)) ** 2.0).astype(jnp.int32), 99999)
        _o = jnp.argsort(dst, stable=True)
        src = src[_o]
        dst = dst[_o]
        edge_weight = jax.random.uniform(jax.random.fold_in(_gk, 12), (200000,), jnp.float32, 0.0, 0.999998)
        return (x, src, dst, edge_weight)
    x, src, dst, edge_weight = _rec_inputs()

    def _L0_gnn_setup():
        import jax, jax.numpy as jnp
        import numpy as np
        N = 12500
        E = 37500
        D = 256

        def _mean_aggregate(x, edge_index, num_nodes):
            src, dst = (edge_index[0], edge_index[1])
            msgs = x[src]
            summed = jax.ops.segment_sum(msgs, dst, num_segments=num_nodes)
            counts = jax.ops.segment_sum(jnp.ones((edge_index.shape[1],), x.dtype), dst, num_segments=num_nodes)
            return summed / jnp.maximum(counts, 1.0)[:, None]
        key = jax.random.key(seed)
        k1, k2, k3, k4, k5, k6 = jax.random.split(key, 6)
        x = jax.random.normal(k1, (N, D), dtype=jnp.float32)
        edge_index = jax.random.randint(k2, (2, E), 0, N, dtype=jnp.int64)
        edge_weight = jax.random.uniform(k3, (E,), dtype=jnp.float32)
        lim = 1.0 / np.sqrt(D)
        W_l = jax.random.uniform(k4, (D, D), dtype=jnp.float32, minval=-lim, maxval=lim)
        b_l = jax.random.uniform(k5, (D,), dtype=jnp.float32, minval=-lim, maxval=lim)
        W_r = jax.random.uniform(k6, (D, D), dtype=jnp.float32, minval=-lim, maxval=lim)
        return {'x': x, 'edge_index': edge_index, 'edge_weight': edge_weight, 'W_l': W_l, 'b_l': b_l, 'W_r': W_r}
    _L0_gnn_all = _L0_gnn_setup()
    _L0_gnn_in = {k: v for k, v in _L0_gnn_all.items() if k in ('W_l', 'b_l', 'W_r')}
    del _L0_gnn_all

    def _L0_mix_setup():
        import jax, jax.numpy as jnp
        import numpy as np
        NHEAD = 8
        ATT_EPS = 1e-06
        LN_EPS = 1e-05

        def _layernorm(x, g, b):
            mu = jnp.mean(x, axis=-1, keepdims=True)
            var = jnp.mean(jnp.square(x - mu), axis=-1, keepdims=True)
            return (x - mu) * jax.lax.rsqrt(var + LN_EPS) * g + b
        key = jax.random.key(seed)
        ks = jax.random.split(key, 7)
        N, L, C = (4, 2048, 256)
        s = 1.0 / np.sqrt(C)
        return {'x': jax.random.normal(ks[0], (N, L, C), jnp.float32), 'Wq': jax.random.normal(ks[1], (C, C), jnp.float32) * s, 'Wk': jax.random.normal(ks[2], (C, C), jnp.float32) * s, 'Wv': jax.random.normal(ks[3], (C, C), jnp.float32) * s, 'Wm': jax.random.normal(ks[4], (C, C), jnp.float32) * s, 'W1': jax.random.normal(ks[5], (2 * C, 2 * C), jnp.float32) * (1.0 / np.sqrt(2 * C)), 'W2': jax.random.normal(ks[6], (2 * C, C), jnp.float32) * (1.0 / np.sqrt(2 * C)), 'g1': jnp.ones((C,), jnp.float32), 'b1': jnp.zeros((C,), jnp.float32), 'g2': jnp.ones((C,), jnp.float32), 'b2': jnp.zeros((C,), jnp.float32)}
    _L0_mix_all = _L0_mix_setup()
    _L0_mix_in = {k: v for k, v in _L0_mix_all.items() if k in ('Wq', 'Wk', 'Wv', 'Wm', 'W1', 'W2', 'g1', 'b1', 'g2', 'b2')}
    del _L0_mix_all

    def _L0_ffn_setup():
        import jax, jax.numpy as jnp
        import numpy as np
        B, S, D = (8, 512, 256)
        H = 4 * D
        CAPACITY = 0.5
        key = jax.random.key(seed)
        ks = jax.random.split(key, 6)
        x = jax.random.normal(ks[0], (B, S, D), dtype=jnp.float32)
        attention_mask = jnp.zeros((B, 1, 1, S), dtype=jnp.float32)
        wr = jax.random.normal(ks[1], (D, 1), dtype=jnp.float32) * 0.02
        br = jnp.zeros((1,), dtype=jnp.float32)
        w1 = jax.random.normal(ks[2], (D, H), dtype=jnp.float32) * 0.02
        b1 = jnp.zeros((H,), dtype=jnp.float32)
        w2 = jax.random.normal(ks[3], (H, D), dtype=jnp.float32) * 0.02
        b2 = jnp.zeros((D,), dtype=jnp.float32)
        return {'x': x, 'attention_mask': attention_mask, 'wr': wr, 'br': br, 'w1': w1, 'b1': b1, 'w2': w2, 'b2': b2}
    _L0_ffn_all = _L0_ffn_setup()
    _L0_ffn_in = {k: v for k, v in _L0_ffn_all.items() if k in ('attention_mask', 'wr', 'br', 'w1', 'b1', 'w2', 'b2')}
    del _L0_ffn_all
    return {'x': x, 'src': src, 'dst': dst, 'edge_weight': edge_weight, 'L0_gnn_W_l': _L0_gnn_in['W_l'], 'L0_gnn_b_l': _L0_gnn_in['b_l'], 'L0_gnn_W_r': _L0_gnn_in['W_r'], 'L0_mix_Wq': _L0_mix_in['Wq'], 'L0_mix_Wk': _L0_mix_in['Wk'], 'L0_mix_Wv': _L0_mix_in['Wv'], 'L0_mix_Wm': _L0_mix_in['Wm'], 'L0_mix_W1': _L0_mix_in['W1'], 'L0_mix_W2': _L0_mix_in['W2'], 'L0_mix_g1': _L0_mix_in['g1'], 'L0_mix_b1': _L0_mix_in['b1'], 'L0_mix_g2': _L0_mix_in['g2'], 'L0_mix_b2': _L0_mix_in['b2'], 'L0_ffn_attention_mask': _L0_ffn_in['attention_mask'], 'L0_ffn_wr': _L0_ffn_in['wr'], 'L0_ffn_br': _L0_ffn_in['br'], 'L0_ffn_w1': _L0_ffn_in['w1'], 'L0_ffn_b1': _L0_ffn_in['b1'], 'L0_ffn_w2': _L0_ffn_in['w2'], 'L0_ffn_b2': _L0_ffn_in['b2']}

def reference(x, src, dst, edge_weight, L0_gnn_W_l, L0_gnn_b_l, L0_gnn_W_r, L0_mix_Wq, L0_mix_Wk, L0_mix_Wv, L0_mix_Wm, L0_mix_W1, L0_mix_W2, L0_mix_g1, L0_mix_b1, L0_mix_g2, L0_mix_b2, L0_ffn_attention_mask, L0_ffn_wr, L0_ffn_br, L0_ffn_w1, L0_ffn_b1, L0_ffn_w2, L0_ffn_b2):
    import jax
    import jax.numpy as jnp

    def _L0_gnn_ref(x, edge_index, edge_weight, W_l, b_l, W_r):
        import jax, jax.numpy as jnp
        import numpy as np
        N = 12500
        E = 37500
        D = 256

        def _mean_aggregate(x, edge_index, num_nodes):
            src, dst = (edge_index[0], edge_index[1])
            msgs = x[src]
            summed = jax.ops.segment_sum(msgs, dst, num_segments=num_nodes)
            counts = jax.ops.segment_sum(jnp.ones((edge_index.shape[1],), x.dtype), dst, num_segments=num_nodes)
            return summed / jnp.maximum(counts, 1.0)[:, None]
        h = x
        agg = _mean_aggregate(x, edge_index, x.shape[0])
        out = agg @ W_l.T + b_l
        out = out + x @ W_r.T
        out = jax.nn.relu(out)
        return out + h

    def _L0_mix_ref(x, Wq, Wk, Wv, Wm, W1, W2, g1, b1, g2, b2):
        import jax, jax.numpy as jnp
        import numpy as np
        NHEAD = 8
        ATT_EPS = 1e-06
        LN_EPS = 1e-05

        def _layernorm(x, g, b):
            mu = jnp.mean(x, axis=-1, keepdims=True)
            var = jnp.mean(jnp.square(x - mu), axis=-1, keepdims=True)
            return (x - mu) * jax.lax.rsqrt(var + LN_EPS) * g + b
        N, L, C = x.shape
        H = NHEAD
        D = C // H
        q = (x @ Wq).reshape(N, L, H, D)
        k = (x @ Wk).reshape(N, L, H, D)
        v = (x @ Wv).reshape(N, L, H, D)
        Q = jax.nn.elu(q) + 1.0
        K = jax.nn.elu(k) + 1.0
        v = v / L
        KV = jnp.einsum('nshd,nshv->nhdv', K, v)
        Z = 1.0 / (jnp.einsum('nlhd,nhd->nlh', Q, K.sum(axis=1)) + ATT_EPS)
        msg = jnp.einsum('nlhd,nhdv,nlh->nlhv', Q, KV, Z) * L
        msg = msg.reshape(N, L, C) @ Wm
        msg = _layernorm(msg, g1, b1)
        h = jnp.concatenate([x, msg], axis=-1) @ W1
        h = jax.nn.relu(h) @ W2
        msg = _layernorm(h, g2, b2)
        return x + msg

    def _L0_ffn_ref(x, attention_mask, wr, br, w1, b1, w2, b2):
        import jax, jax.numpy as jnp
        import numpy as np
        B, S, D = (8, 512, 256)
        H = 4 * D
        CAPACITY = 0.5
        b, s, d = x.shape
        weights = (jnp.einsum('bsd,do->bso', x, wr) + br)[..., 0]
        k = max(1, int(CAPACITY * s))
        kk = k - 1 if k > 1 else 1
        _, idx = jax.lax.top_k(weights, k)
        sel_idx = idx[:, :kk]
        sel = jnp.take_along_axis(x, sel_idx[:, :, None], axis=1)
        h = jax.nn.gelu(jnp.einsum('bkd,dh->bkh', sel, w1) + b1)
        y = jnp.einsum('bkh,hd->bkd', h, w2) + b2
        w_sel = jnp.take_along_axis(weights, sel_idx, axis=1)
        y = y * w_sel[..., None]
        batch_idx = jnp.arange(b)[:, None]
        processed = jnp.zeros_like(x).at[batch_idx, sel_idx].set(y)
        return processed + x
    edge_index = jnp.stack([src, dst])
    xn = _layernorm(x, axis=-1)
    x = x + _L0_gnn_ref(xn, edge_index, edge_weight, L0_gnn_W_l, L0_gnn_b_l, L0_gnn_W_r) + _L0_mix_ref(xn[None], L0_mix_Wq, L0_mix_Wk, L0_mix_Wv, L0_mix_Wm, L0_mix_W1, L0_mix_W2, L0_mix_g1, L0_mix_b1, L0_mix_g2, L0_mix_b2)[0]
    x = x + _L0_ffn_ref(_layernorm(x, axis=-1)[None], L0_ffn_attention_mask, L0_ffn_wr, L0_ffn_br, L0_ffn_w1, L0_ffn_b1, L0_ffn_w2, L0_ffn_b2)[0]
    return x

_drawn_inputs = setup_inputs


def setup_inputs(seed=0):
    import zlib

    import numpy as np

    out = dict(_drawn_inputs(seed))
    spreads = {'L0_mix_g1': (1.0, 0.2),
     'L0_mix_b1': (0.0, 0.359),
     'L0_mix_g2': (1.0, 0.2),
     'L0_mix_b2': (0.0, 0.1),
     'L0_ffn_b1': (0.0, 0.8),
     'L0_ffn_b2': (0.0, 0.8)}
    factors = {'L0_gnn_b_l': 7.236, 'L0_ffn_wr': 8.0, 'L0_ffn_w1': 8.0, 'L0_ffn_w2': 8.0}
    for name, (base, spread) in spreads.items():
        noise = np.random.default_rng([zlib.crc32(name.encode()), seed]).standard_normal(out[name].shape)
        drawn = base * np.exp(spread * noise) if base else spread * noise
        out[name] = jnp.asarray(drawn.astype(out[name].dtype))
    for name, factor in factors.items():
        out[name] = (out[name] * factor).astype(out[name].dtype)
    return out
```

```python
import numpy as np
import concourse.bass as bass
from concourse import mybir
from contextlib import ExitStack

f32 = mybir.dt.float32
f16 = mybir.dt.float16
i32 = mybir.dt.int32
ALU = mybir.AluOpType
ACT = mybir.ActivationFunctionType
AX = mybir.AxisListType

P = 128
N, D, E = 12500, 256, 200000
NBLK = -(-N // P)
NPAD = NBLK * P
LASTROWS = N - (NBLK - 1) * P
NSUP = NBLK // 2
SB = 2 * P
TPG = 4
GE = TPG * P
KG, MG = 2, 6
NG = NSUP * (KG + MG)
RING = 6
FULLG, RESTE = E // GE, E % GE
CH = -(-NG // P)
LASTC = FULLG - (CH - 1) * P
PADNODE = NPAD - 1
HEADS = 8
DH = D // HEADS
LN_EPS, ATT_EPS = 1e-5, 1e-6
HF = 4 * D
KK = max(1, N // 2) - 1
NSEL = -(-KK // P)
LASTSEL = KK - (NSEL - 1) * P
BPB = 7
NBATCH = NBLK // BPB
GROW = 2 * D + 4
AGW = D + 1

assert NBLK % 2 == 0 and NBLK % BPB == 0 and NG * GE >= E and NG <= CH * P
assert 0 < LASTC < P and KG * 3 == RING and MG == RING


def past(i, k):
    return not isinstance(i, int) or i >= k


def steps(eng, body, n, unroll, tail=0):
    for i in range(min(unroll, n)):
        body(i, i, 0)
    end = (n - tail) // unroll
    if end > 1:
        with eng.Fori(1, end) as j:
            for s in range(unroll):
                body(j * unroll + s, s, j)
    for i in range(max(end, 1) * unroll, n):
        body(i, i % unroll, i // unroll)


def alone(eng, stood):
    eng.sem_inc(stood, 1)


class Chain:

    def __init__(self, eng, sem):
        self.eng, self.sem, self.base, self.n = eng, sem, 0, 0

    def at(self, base):
        self.base, self.n = base, 0

    def link(self, ins):
        self.n += 1
        ins.then_inc(self.sem, 1)
        self.eng.wait_ge(self.sem, self.base + self.n)


def build(nc, x, src, dst, W_l, b_l, W_r, Wq, Wk, Wv, Wm, W1, W2, g1, b1, g2, b2, wr, br, w1, fb1, w2, fb2, out):
    ds = bass.ds
    ctx = ExitStack()
    with ctx:
        def sb(name, shape, dt=f32):
            return ctx.enter_context(nc.sbuf_tensor(name, shape, dt))

        def sem(name):
            return ctx.enter_context(nc.semaphore(name))

        xtab = nc.dram_tensor("xtab", (NPAD, 2 * D), f16, kind="Internal").ap()
        bounds_d = nc.dram_tensor("bounds_d", (CH * P, 2), i32, kind="Internal").ap()
        q_d = nc.dram_tensor("q_d", (NSUP, P, 2 * SB), f32, kind="Internal").ap()
        rg_d = nc.dram_tensor("rg_d", (NPAD, 2 * D), f32, kind="Internal").ap()
        ff_d = nc.dram_tensor("ff_d", (NPAD, 2 * D), f32, kind="Internal").ap()

        def rows(t, i, n=2):
            return t.rearrange("(b p) c -> p b c", p=P)[:, ds(i, n) if not isinstance(i, int) else slice(i, i + n), :]

        agg = sb("agg", [P, NBLK, AGW])
        gath_raw = sb("gath_raw", [P, RING * TPG * GROW // 2])
        gath = gath_raw[:, :].bitcast(f16).rearrange("p (s c) -> p s c", c=GROW)
        edges_i = gath_raw[:, 0:2 * CH * GE].bitcast(i32).rearrange("p (a c e) -> p a c e", a=2, c=CH)
        edges_f = gath_raw[:, 0:2 * CH * GE].rearrange("p (a c e) -> p a c e", a=2, c=CH)
        wq_s = sb("wq_s", [P, 2, D])
        wkv_s = sb("wkv_s", [P, 2, 2 * D])
        wm_s = sb("wm_s", [P, 2, D])
        w1_s = sb("w1_s", [P, 4, 2 * D])
        w2_s = sb("w2_s", [P, 4, D])
        wlr_n = gath_raw[:, 2 * CH * GE:2 * CH * GE + 4 * D].rearrange("p (a n) -> p a n", n=D)
        wlT = sb("wlT", [P, 2, D])
        wrT = sb("wrT", [P, 2, D])
        dstF = sb("dstF", [P, NG, TPG])
        srcI = sb("srcI", [P, NG, TPG], i32)
        rstd = sb("rstd", [P, NBLK])
        nmr = sb("nmr", [P, NBLK])
        res_s = sb("res_s", [P, NBLK])
        res_b = sb("res_b", [P, NBLK])
        wtok = sb("wtok", [P, NBLK])
        bl_s = sb("bl_s", [P, D])
        g2_s = sb("g2_s", [P, D])
        b2_s = sb("b2_s", [P, D])
        fb2_s = sb("fb2_s", [P, D])
        wr_s = sb("wr_s", [P, D])
        br_s = sb("br_s", [P, 1])
        g1_s = sb("g1_s", [P, 2])
        b1_s = sb("b1_s", [P, 2])
        fb1_s = sb("fb1_s", [P, HF // P])
        ident = sb("ident", [P, P])
        ones = sb("ones", [P, P])
        tri = sb("tri", [P, P])
        headm = sb("headm", [P, P])
        iota16 = sb("iota16", [P, P], f16)
        iotaf = sb("iotaf", [P, P])
        blkbase = sb("blkbase", [P, NBLK])
        pcol = sb("pcol", [P, 1])
        lastvalid = sb("lastvalid", [P, 1])
        onehot = sb("onehot", [P, 2, TPG, P], f16)
        stage = sb("stage", [P, 2, RING, TPG], i32)
        bnd = sb("bnd", [1, 2 * NG], i32)
        kvbd = sb("kvbd", [P, 2, P])
        ksbd = sb("ksbd", [P, 2, P])
        rcnt = sb("rcnt", [P, NBLK])
        small_i = sb("small_i", [P, 2 * CH], i32)
        stats = sb("stats", [P, BPB, 6])
        mv = sb("mv", [P, BPB, 2])
        small = sb("small", [P, 64])
        work = sb("work", [P, 7680])

        def part(base, a, shape):
            n = int(np.prod(shape))
            v = base[:, a:a + n]
            if len(shape) == 2:
                v = v.rearrange("p (a b) -> p a b", a=shape[0])
            if len(shape) == 3:
                v = v.rearrange("p (a b c) -> p a b c", a=shape[0], b=shape[1])
            return v

        ps = ctx.enter_context(nc.psum_tensor("ps", [P, 8, 512], f32))
        BA, BB, BC, BD, BE, BF, BG = range(7)

        def bank(b, shape=(2, 256)):
            return part(ps[:, b, :], 0, shape)

        cst = sem("cst")
        stood = sem("stood")
        wts_in = sem("wts_in")
        wlr_in = sem("wlr_in")
        ffw_in = sem("ffw_in")
        edges_in = sem("edges_in")
        edges_pad = sem("edges_pad")
        edges_cast = sem("edges_cast")
        tr_ps = sem("tr_ps")
        tr_ev = sem("tr_ev")
        bnd_out = sem("bnd_out")
        bnd_in = sem("bnd_in")
        bnd_ready = sem("bnd_ready")
        agg_zero = sem("agg_zero")
        ln_x_in = [sem(f"ln_x_in{i}") for i in range(2)]
        ln_var = sem("ln_var")
        ln_rstd = sem("ln_rstd")
        ln_nmr = sem("ln_nmr")
        ln_xn = sem("ln_xn")
        ln_hi = sem("ln_hi")
        ln_lo = sem("ln_lo")
        ln_tab = sem("ln_tab")
        res_set = sem("res_set")
        ln_out = [sem(f"ln_out{i}") for i in range(2)]
        own_dve = sem("own_dve")
        own_act = sem("own_act")
        oh_ready = sem("oh_ready")
        seg_done = sem("seg_done")
        seg_added = sem("seg_added")
        grp_used = sem("grp_used")
        rows_in = [sem(f"rows_in{i}") for i in range(RING)]
        ones_set = sem("ones_set")
        stage_set = sem("stage_set")
        k_x_in = [sem(f"k_x_in{i}") for i in range(3)]
        k_xn = sem("k_xn")
        k_xT_ps = sem("k_xT_ps")
        k_xnT = sem("k_xnT")
        k_kv_ps = sem("k_kv_ps")
        k_q_ps = sem("k_q_ps")
        k_kmin = sem("k_kmin")
        k_qmin = sem("k_qmin")
        k_kexp = sem("k_kexp")
        k_qexp = sem("k_qexp")
        k_v = sem("k_v")
        k_K = sem("k_K")
        k_Q = sem("k_Q")
        k_acc = sem("k_acc")
        k_ones = sem("k_ones")
        q_out = [sem(f"q_out{i}") for i in range(3)]
        kvbd_set = sem("kvbd_set")
        m_x_in = [sem(f"m_x_in{i}") for i in range(2)]
        m_q_in = [sem(f"m_q_in{i}") for i in range(2)]
        m_xn = sem("m_xn")
        m_xs = sem("m_xs")
        m_nd_ps = sem("m_nd_ps")
        m_xT_ps = sem("m_xT_ps")
        m_xnT = sem("m_xnT")
        m_msg = sem("m_msg")
        m_y_ps = sem("m_y_ps")
        m_v1 = sem("m_v1")
        m_r1 = sem("m_r1")
        m_yn = sem("m_yn")
        m_gr_ps = sem("m_gr_ps")
        m_gr = sem("m_gr")
        m_yT_ps = sem("m_yT_ps")
        m_ynT = sem("m_ynT")
        m_h1_ps = sem("m_h1_ps")
        m_h1 = sem("m_h1")
        m_h2_ps = sem("m_h2_ps")
        m_v2 = sem("m_v2")
        m_r2 = sem("m_r2")
        m_n2 = sem("m_n2")
        m_r = sem("m_r")
        rg_out = [sem(f"rg_out{i}") for i in range(2)]
        g_in = [sem(f"g_in{i}") for i in range(2)]
        g_ma = sem("g_ma")
        g_T_ps = sem("g_T_ps")
        g_aT = sem("g_aT")
        g_ps = sem("g_ps")
        g_s = sem("g_s")
        g_v = sem("g_v")
        g_r = sem("g_r")
        g_xn = sem("g_xn")
        g_base = sem("g_base")
        g_w = sem("g_w")
        ff_out = [sem(f"ff_out{i}") for i in range(2)]
        s_cnt = sem("s_cnt")
        s_tot = sem("s_tot")
        s_a = sem("s_a")
        s_mm = sem("s_mm")
        s_idx = sem("s_idx")
        fstage = [sem(f"fstage{i}") for i in range(2)]
        f_in = [sem(f"f_in{i}") for i in range(2)]
        f_T_ps = sem("f_T_ps")
        f_xT = sem("f_xT")
        f_h_ps = sem("f_h_ps")
        f_h = sem("f_h")
        f_y_ps = sem("f_y_ps")
        f_w = sem("f_w")
        f_yb = sem("f_yb")
        f_o = sem("f_o")
        f_out = [sem(f"f_out{i}") for i in range(2)]

        ln_x = [part(work, s * BPB * D, (BPB, D)) for s in range(2)]
        ln_n = part(work, 2 * BPB * D, (BPB, D))
        ln_t = [gath_raw[:, s * BPB * D:(s + 1) * BPB * D].bitcast(f16).rearrange("p (b c) -> p b c", c=2 * D)
                for s in range(2)]
        ln_ve, ln_rc, ln_rs, ln_nm = (small[:, 8 * i:8 * i + BPB] for i in range(4))
        kx = [part(work, 512 * s, (2, D)) for s in range(3)]
        kxn = part(work, 1536, (2, D))
        kxT = [part(work, 2048 + 512 * s, (2, SB)) for s in range(3)]
        kmin = part(work, 3584, (2, D))
        kk_s = part(work, 4096, (2, D))
        vaug = part(work, 4608, (2, 2, P + 1))
        qmin = part(work, 5136, (2, SB))
        qout = [part(work, 5648 + 512 * s, (2, SB)) for s in range(3)]
        mx = [part(work, 512 * s, (2, D)) for s in range(2)]
        mxn = part(work, 1024, (2, D))
        mxT = [part(work, 1536 + 512 * s, (2, SB)) for s in range(2)]
        mq = [part(work, 2560 + 512 * s, (2, SB)) for s in range(2)]
        mmsg = mynT = part(work, 3584, (2, SB))
        myn = mn2 = mden = part(work, 4096, (2, D))
        mh1 = part(work, 4608, (4, SB))
        mrg = [part(work, 5632 + 1024 * s, (2, 2 * D)) for s in range(2)]
        grg = [part(work, 1024 * s, (2, 2 * D)) for s in range(2)]
        gma = part(work, 2048, (2, D))
        gaT = part(work, 2560, (2, SB))
        gs = part(work, 3072, (2, D))
        gx1 = part(work, 3584, (2, D))
        gff = [part(work, 4096 + 1024 * s, (2, 2 * D)) for s in range(2)]
        pool2 = agg[:, :, :].rearrange("p b c -> p (b c)")
        s_gt, s_eq, s_rank, s_junk, s_colf = (pool2[:, 128 * k:128 * k + NBLK] for k in range(5))
        s_pos, s_q = (pool2[:, 128 * k:128 * k + NBLK].bitcast(i32) for k in (5, 6))
        s_sum = [pool2[:, 128 * k:128 * k + NBLK] for k in (7, 8)]
        s_prefix, s_bit, s_cand, s_m, s_f = (pool2[:, 1152 + k:1153 + k].bitcast(i32) for k in range(5))
        s_count = pool2[:, 1160:1161]
        sel_idx = pool2[:, 1168:1168 + NSEL].bitcast(i32)
        s_oh = [pool2[:, 1280 + 64 * k:1344 + 64 * k].bitcast(f16) for k in range(3)]
        s_pc = [pool2[:, 1536 + 64 * k:1536 + 64 * k + NSEL].bitcast(f16) for k in range(3)]
        fstg = [pool2[:, 1760 + 2 * k:1762 + 2 * k].bitcast(i32) for k in range(2)]
        frow = [part(pool2, 2048 + 1024 * k, (2, 2 * D)) for k in range(2)]
        f_xTs = [part(pool2, 4096 + 512 * k, (2, SB)) for k in range(2)]
        fh = part(pool2, 5120, (HF // P, SB))
        f_junk = part(pool2, 7168, (2, D))
        fo = [part(pool2, 7680 + 512 * k, (2, D)) for k in range(2)]
        fw1_s = part(pool2, 9216, (2, HF))
        fw2_s = part(pool2, 9216 + 2 * HF, (HF // P, D))

        def seg_values(eng, etype, g0, n, prev):
            a = 2 * g0 - (1 if prev else 0)
            k = 2 * n + (1 if prev else 0)
            ap = bnd[0:1, a:a + k] if isinstance(g0, int) else bnd[0:1, ds(a, k)]
            _, v = nc.values_load_multi_w_load_instructions(
                ap, engines=[etype], min_val=0, max_val=NBLK - 1,
                skip_runtime_bounds_check_because="block numbers of node numbers below NPAD")
            v = list(v)
            before = v.pop(0) if prev else None
            return before, [(v[2 * t], v[2 * t + 1]) for t in range(n)]


        def k_place(s, j, t):
            return KG * s + t, j

        def m_place(i, t):
            g = KG * NSUP + t
            return g % RING, g // RING + i

        def bcast(v, n):
            return v.unsqueeze(1).to_broadcast([P, n, D])

        block = ctx.enter_context(nc.Block())

        @block.sync
        def _(e):
            for a, t in ((0, src), (1, dst)):
                e.dma_start(edges_i[:, a, 0:CH - 1, :],
                            t[0:(CH - 1) * P * GE].rearrange("(c p e) -> p c e", p=P, e=GE)).then_inc(edges_in, 16)
            e.wait_ge(edges_pad, 2)
            o = (CH - 1) * P * GE
            for a, t in ((0, src), (1, dst)):
                e.dma_start(edges_i[0:LASTC, a, CH - 1, :],
                            t[o:FULLG * GE].rearrange("(p e) -> p e", e=GE)).then_inc(edges_in, 16)
                e.dma_start(edges_i[LASTC:LASTC + 1, a, CH - 1, 0:RESTE],
                            t[FULLG * GE:E].rearrange("(p e) -> p e", p=1)).then_inc(edges_in, 16)

            def ln_io(m, s, j):
                if past(m, 2):
                    e.wait_ge(ln_xn, m - 1)
                e.dma_start(ln_x[s], rows(x, m * BPB, BPB)).then_inc(ln_x_in[s], 16)
                if past(m, 1):
                    e.wait_ge(ln_lo, m)
                    e.wait_ge(ln_hi, m)
                    e.dma_start(rows(xtab, (m - 1) * BPB, BPB), ln_t[1 - s]).then_inc(ln_out[1 - s], 16)
            steps(e, ln_io, NBATCH, 2)
            e.wait_ge(ln_lo, NBATCH)
            e.wait_ge(ln_hi, NBATCH)
            e.dma_start(rows(xtab, (NBATCH - 1) * BPB, BPB), ln_t[(NBATCH - 1) % 2]).then_inc(ln_out[(NBATCH - 1) % 2], 16)

            e.wait_ge(bnd_ready, 1)
            e.dma_start(bounds_d.rearrange("(c p) k -> p c k", p=P),
                        small_i[:, 0:2 * CH].rearrange("p (c k) -> p c k", k=2)).then_inc(bnd_out, 16)
            e.wait_ge(bnd_out, 16)
            e.dma_start(bnd[0:1, :], bounds_d[0:NG, :].rearrange("(o g) k -> o (g k)", o=1)).then_inc(bnd_in, 16)

            e.wait_ge(ln_out[0], 16 * (NBATCH // 2))
            e.wait_ge(ln_out[1], 16 * (NBATCH // 2))
            e.dma_start(kx[0], rows(x, 0)).then_inc(k_x_in[0], 16)

            def k_io(i, s, j):
                if not (isinstance(i, int) and i == NSUP - 1):
                    if past(i, 2):
                        e.wait_ge(k_xn, i - 1)
                    e.dma_start(kx[(s + 1) % 3], rows(x, 2 * i + 2)).then_inc(k_x_in[(s + 1) % 3], 16)
                e.wait_ge(k_Q, i + 1)
                e.dma_start(q_d[ds(i, 1) if not isinstance(i, int) else slice(i, i + 1), :, :].rearrange("o p c -> p (o c)"),
                            qout[s].rearrange("p a b -> p (a b)")).then_inc(q_out[s], 16)
            steps(e, k_io, NSUP, 3)
            for s in range(3):
                e.wait_ge(q_out[s], 16 * len(range(s, NSUP, 3)))
            e.wait_ge(k_acc, NSUP)

            def m_load(i, s):
                q = q_d[ds(i, 1) if not isinstance(i, int) else slice(i, i + 1), :, :]
                e.dma_start(mx[s], rows(x, 2 * i)).then_inc(m_x_in[s], 16)
                e.dma_start(mq[s].rearrange("p a b -> p (a b)"), q.rearrange("o p c -> p (o c)")).then_inc(m_q_in[s], 16)
            m_load(0, 0)

            def m_io(i, s, j):
                if not (isinstance(i, int) and i == NSUP - 1):
                    if past(i, 1):
                        e.wait_ge(m_xs, i)
                        e.wait_ge(m_nd_ps, i)
                    m_load(i + 1, 1 - s)
                e.wait_ge(m_r, i + 1)
                e.dma_start(rows(rg_d, 2 * i), mrg[s]).then_inc(rg_out[s], 16)
            steps(e, m_io, NSUP, 2)
            for s in range(2):
                e.wait_ge(rg_out[s], 16 * len(range(s, NSUP, 2)))

            e.dma_start(grg[0], rows(rg_d, 0)).then_inc(g_in[0], 16)

            def g_io(i, s, j):
                if not (isinstance(i, int) and i == NSUP - 1):
                    if past(i, 1):
                        e.wait_ge(g_s, i)
                    e.dma_start(grg[1 - s], rows(rg_d, 2 * i + 2)).then_inc(g_in[1 - s], 16)
                e.wait_ge(g_base, i + 1)
                e.dma_start(rows(ff_d, 2 * i), gff[s]).then_inc(ff_out[s], 16)
                e.dma_start(rows(out, 2 * i), gff[s][:, :, D:2 * D]).then_inc(ff_out[s], 16)
            steps(e, g_io, NSUP, 2)
            e.dma_start(fw1_s, w1.rearrange("(k p) n -> p k n", p=P)).then_inc(ffw_in, 16)
            e.dma_start(fw2_s, w2.rearrange("(k p) n -> p k n", p=P)).then_inc(ffw_in, 16)
            for s in range(2):
                e.wait_ge(ff_out[s], 32 * len(range(s, NSUP, 2)))
                e.wait_ge(f_out[s], 32 * len(range(s, NSEL // 2, 2)) + (16 if NSEL // 2 % 2 == s else 0))

        @block.gpsimd
        def _(e):
            e.memset(edges_i[:, 0, CH - 1, :], 0).then_inc(edges_pad, 1)
            e.memset(edges_i[:, 1, CH - 1, :], PADNODE).then_inc(edges_pad, 1)
            e.memset(ones[:, :], 1.0).then_inc(cst, 1)
            e.memset(ident[:, :], 0.0).then_inc(cst, 1)
            e.wait_ge(cst, 2)
            e.affine_select(out=ident[:, :], in_=ident[:, :], compare_op=ALU.not_equal, fill=1.0,
                            base=0, pattern=[[-1, P]], channel_multiplier=1).then_inc(cst, 1)
            e.affine_select(out=tri[:, :], in_=ones[:, :], compare_op=ALU.is_gt, fill=0.0,
                            base=0, pattern=[[1, P]], channel_multiplier=-1).then_inc(cst, 1)
            hm = headm[:, :].rearrange("p (h d) -> p h d", d=DH)
            e.affine_select(out=hm, in_=ones[:, :].rearrange("p (h d) -> p h d", d=DH), compare_op=ALU.is_ge, fill=0.0,
                            base=0, pattern=[[-DH, P // DH], [0, DH]], channel_multiplier=1).then_inc(cst, 1)
            e.wait_ge(cst, 5)
            e.affine_select(out=hm, in_=hm, compare_op=ALU.is_ge, fill=0.0,
                            base=DH - 1, pattern=[[DH, P // DH], [0, DH]], channel_multiplier=-1).then_inc(cst, 1)
            e.affine_select(out=lastvalid[:, :], in_=ones[:, 0:1], compare_op=ALU.is_gt, fill=0.0,
                            base=LASTROWS, pattern=[[0, 1]], channel_multiplier=-1).then_inc(cst, 1)
            e.iota(iota16[:, :], pattern=[[1, P]], base=0, channel_multiplier=0,
                   allow_small_or_imprecise_dtypes=True).then_inc(cst, 1)
            e.iota(iotaf[:, :], pattern=[[1, P]], base=0, channel_multiplier=0,
                   allow_small_or_imprecise_dtypes=True).then_inc(cst, 1)
            e.iota(blkbase[:, :], pattern=[[P, NBLK]], base=0, channel_multiplier=0,
                   allow_small_or_imprecise_dtypes=True).then_inc(cst, 1)
            e.iota(pcol[:, :], pattern=[[0, 1]], base=0, channel_multiplier=1,
                   allow_small_or_imprecise_dtypes=True).then_inc(cst, 1)
            for b in range(0, NBLK, 14):
                e.memset(agg[:, b:b + 14, :], 0.0).then_inc(agg_zero, 1)

            e.wait_ge(edges_cast, 2)
            e.wait_ge(tr_ps, 2 * CH + 2)

            def ln_high(m, s, j):
                e.wait_ge(ln_xn, m + 1)
                if past(m, 2):
                    e.wait_ge(ln_out[s], 16 * j)
                alone(e, stood)
                e.tensor_copy(ln_t[s][:, :, 0:D], ln_n).then_inc(ln_hi, 1)
            steps(e, ln_high, NBATCH, 2)

            e.wait_ge(tr_ev, 2 * CH)
            e.wait_ge(ln_out[0], 16 * (NBATCH // 2))
            e.wait_ge(ln_out[1], 16 * (NBATCH // 2))
            e.memset(gath[:, :, 2 * D:2 * D + 1], 1.0).then_inc(ones_set, 1)

            def gather(i, h, n):
                c = srcI[:, ds(RING * i, n), :] if not isinstance(i, int) else srcI[:, RING * i:RING * i + n, :]
                e.tensor_copy(stage[:, h, 0:n, :], c).then_inc(stage_set, 1)
                e.wait_ge(stage_set, i + 1)
                alone(e, stood)
                for s in range(n):
                    if past(i, 1):
                        e.wait_ge(grp_used, RING * (i - 1) + s + 1)
                        alone(e, stood)
                    for t in range(TPG):
                        e.indirect_dma_start(
                            out=gath[:, TPG * s + t, 0:2 * D], out_offset=None, in_=xtab[:, :],
                            in_offset=bass.IndirectOffsetOnAxis(ap=stage[:, h, s, t:t + 1], axis=0)
                        ).then_inc(rows_in[s], 16)
            steps(e, lambda i, h, j: gather(i, h, RING), NG // RING, 2)
            gather(NG // RING, NG // RING % 2, NG % RING)

            e.wait_ge(s_idx, 1)
            for s in range(2):
                e.wait_ge(ff_out[s], 32 * len(range(s, NSUP, 2)))

            def f_gather(i, s, n):
                c = sel_idx[:, ds(2 * i, n)] if not isinstance(i, int) else sel_idx[:, 2 * i:2 * i + n]
                e.tensor_copy(fstg[s][:, 0:n], c).then_inc(fstage[s], 1)

            def f_io(i, s, j):
                n = 1 if isinstance(i, int) and i == NSEL // 2 else 2
                if past(i, 2):
                    e.wait_ge(f_out[s], 32 * j)
                    alone(e, stood)
                f_gather(i, s, n)
                e.wait_ge(fstage[s], j + 1)
                alone(e, stood)
                for u in range(n):
                    e.indirect_dma_start(out=frow[s][:, u, :], out_offset=None, in_=ff_d[:, :],
                                         in_offset=bass.IndirectOffsetOnAxis(ap=fstg[s][:, u:u + 1], axis=0)
                                         ).then_inc(f_in[s], 16)
                if past(i, 1):
                    scatter(i - 1, 1 - s, 2, P)

            def scatter(i, s, n, r):
                e.wait_ge(f_o, i + 1)
                alone(e, stood)
                for u in range(n):
                    e.indirect_dma_start(out=out[:, :], in_=fo[s][0:r, u, :], in_offset=None,
                                         out_offset=bass.IndirectOffsetOnAxis(ap=fstg[s][0:r, u:u + 1], axis=0)
                                         ).then_inc(f_out[s], 16)
            steps(e, f_io, NSEL // 2 + 1, 2, 2)
            scatter(NSEL // 2, NSEL // 2 % 2, 1, LASTSEL)

        @block.vector
        def _(e):
            v = nc.vector
            own = Chain(e, own_dve)
            pair = e.alloc_register("dve_pair")
            e.reg_mov(pair, 0)

            v.memset(small[:, 40:41], 0.0).then_inc(seg_added, 2)
            v.memset(small[:, 41:42], 0.0).then_inc(seg_done, 2)

            e.wait_ge(edges_in, 96)
            e.wait_ge(edges_pad, 2)
            for a in range(2):
                v.tensor_copy(edges_f[:, a, :, :], edges_i[:, a, :, :]).then_inc(edges_cast, 1)
            e.wait_ge(edges_cast, 2)
            lo_hi = small[:, 48:48 + 2 * CH].rearrange("p (c k) -> p c k", k=2)
            v.tensor_reduce(lo_hi[:, :, 0], edges_f[:, 1, :, :], AX.X, ALU.min).then_inc(own_dve, 1)
            v.tensor_reduce(lo_hi[:, :, 1], edges_f[:, 1, :, :], AX.X, ALU.max).then_inc(own_dve, 1)
            e.wait_ge(own_dve, 2)
            own.at(2)
            own.link(v.tensor_copy(small_i[:, 0:2 * CH], small[:, 48:48 + 2 * CH]))
            v.tensor_scalar(small_i[:, 0:2 * CH], small_i[:, 0:2 * CH], 7, None, ALU.arith_shift_right
                            ).then_inc(bnd_ready, 1)
            for c in range(CH):
                n = min(P, NG - c * P)
                e.wait_ge(tr_ps, CH + c + 1)
                v.tensor_copy(dstF[:, c * P:c * P + n, :],
                              bank((CH + c) % 8, (TPG, P)).rearrange("p t g -> p g t")[:, 0:n, :]).then_inc(tr_ev, 1)
            e.wait_ge(tr_ps, 2 * CH + 2)
            v.tensor_copy(wlT[:, :, :], bank(0)).then_inc(tr_ev, 1)
            v.tensor_copy(wrT[:, :, :], bank(1)).then_inc(tr_ev, 1)

            def ln_stats(m, s, j):
                own.at(3 + 2 * m)
                e.wait_ge(ln_x_in[s], 16 * j + 16)
                for k in range(BPB):
                    last = v.bn_stats(stats[:, k, :], ln_x[s][:, k, :])
                own.link(last)
                alone(e, stood)
                for k in range(BPB):
                    last = v.bn_aggr(mv[:, k, :], stats[:, k, :])
                own.link(last)
                ln_step(m)

            def ln_step(m):
                v.tensor_scalar(ln_ve, mv[:, :, 1], LN_EPS, None, ALU.add).then_inc(ln_var, 1)
                e.wait_ge(ln_var, 2 * m + 1)
                v.reciprocal(ln_rc, ln_ve).then_inc(ln_var, 1)
                e.wait_ge(ln_rstd, m + 1)
                v.scalar_tensor_tensor(out=ln_nm, in0=mv[:, :, 0], scalar=-1.0, in1=ln_rs,
                                       op0=ALU.mult, op1=ALU.mult).then_inc(ln_nmr, 1)
                e.wait_ge(ln_nmr, m + 1)
                cols = (lambda t: t[:, m * BPB:m * BPB + BPB] if isinstance(m, int) else t[:, ds(m * BPB, BPB)])
                v.tensor_copy(cols(rstd), ln_rs)
                v.tensor_copy(cols(nmr), ln_nm).then_inc(ln_tab, 1)

            def ln_low(m, s, j):
                e.wait_ge(ln_hi, m + 1)
                v.tensor_tensor(ln_t[s][:, :, D:2 * D], ln_n, ln_t[s][:, :, 0:D], ALU.subtract).then_inc(ln_lo, 1)

            def ln_body(m, s, j):
                ln_stats(m, s, j)
                ln_low(m, s, j)
            steps(e, ln_body, NBATCH, 2)
            e.wait_ge(ln_tab, NBATCH)
            v.tensor_scalar(res_s[:, :], rstd[:, :], 2.0, 1.0, ALU.mult, ALU.add).then_inc(res_set, 1)
            v.tensor_scalar(res_b[:, :], nmr[:, :], 2.0, None, ALU.mult).then_inc(res_set, 1)
            e.wait_ge(ln_out[0], 16 * (NBATCH // 2))
            e.wait_ge(ln_out[1], 16 * (NBATCH // 2))
            v.memset(vaug[:, :, :, P:P + 1], 1.0).then_inc(k_ones, 1)

            e.wait_ge(cst, 11)
            e.wait_ge(agg_zero, NBLK // 14)
            e.wait_ge(bnd_in, 16)
            e.wait_ge(tr_ev, 2 * CH)

            def one_hot(g, b, p):
                e.wait_ge(seg_done, p + 1)
                for t in range(TPG):
                    c = dstF[:, g:g + 1, t] if isinstance(g, int) else dstF[:, ds(g, 1), t]
                    last = v.tensor_scalar(onehot[:, ds(p % 2, 1), t, :], iota16[:, :],
                                           blkbase[:, ds(b, 1)], c, ALU.add, ALU.is_equal)
                last.then_inc(oh_ready, 1)

            def add_before(b, p):
                e.wait_ge(seg_done, p + 2)
                v.tensor_tensor(agg[:, ds(b, 1), :], agg[:, ds(b, 1), :],
                                ps[:, ds(BG + (p + 1) % 2, 1), 0:AGW], ALU.add).then_inc(seg_added, 1)

            def seg(g, before, first, last):
                p = e.snap(pair)
                one_hot(g, first, p)
                if before is not None:
                    add_before(before, p)
                    e.wait_ge(seg_added, p + 2)
                    e.sem_inc(grp_used, 1)
                e.reg_add(pair, pair, 1)
                with e.If(first < last):
                    with e.Fori(first + 1, last + 1) as b:
                        q = e.snap(pair)
                        one_hot(g, b, q)
                        add_before(b - 1, q)
                        e.reg_add(pair, pair, 1)

            def k_body(i, s, j):
                before, spans = seg_values(e, mybir.EngineType.DVE, KG * i, KG, past(i, 1))
                seg(KG * i, before, *spans[0])
                e.wait_ge(k_kv_ps, i + 1)
                v.tensor_scalar(kmin, bank(BC), 0.0, None, ALU.min).then_inc(k_kmin, 1)
                e.wait_ge(k_q_ps, i + 1)
                v.tensor_scalar(qmin, bank(BB), 0.0, None, ALU.min).then_inc(k_qmin, 1)
                seg(KG * i + 1, spans[0][1], *spans[1])
                e.wait_ge(k_kexp, i + 1)
                if past(i, 1):
                    e.wait_ge(k_acc, i)
                v.scalar_tensor_tensor(out=kk_s, in0=bank(BC), scalar=0.0, in1=kmin,
                                       op0=ALU.max, op1=ALU.add).then_inc(k_K, 1)
                e.wait_ge(k_qexp, i + 1)
                if past(i, 3):
                    e.wait_ge(q_out[s], 16 * j)
                v.scalar_tensor_tensor(out=qout[s], in0=bank(BB), scalar=0.0, in1=qmin,
                                       op0=ALU.max, op1=ALU.add).then_inc(k_Q, 1)
            steps(e, k_body, NSUP, 3)

            e.wait_ge(k_acc, NSUP)
            for c in range(2):
                a = ps[:, BE, c * (P + 1):c * (P + 1) + P]
                v.scalar_tensor_tensor(out=kvbd[:, c, :], in0=a, scalar=1.0 / N, in1=headm[:, :],
                                       op0=ALU.mult, op1=ALU.mult)
                last = v.tensor_copy(small[:, 42 + c:43 + c], ps[:, BE, c * (P + 1) + P:(c + 1) * (P + 1)])
            last.then_inc(kvbd_set, 1)
            e.wait_ge(kvbd_set, 1)
            for c in range(2):
                last = v.tensor_scalar(ksbd[:, c, :], headm[:, :], small[:, 42 + c:43 + c], None, ALU.mult)
            last.then_inc(kvbd_set, 1)

            def norm_stats(src_ps, var_sem, i, base):
                own.at(base)
                for u in range(2):
                    last = v.bn_stats(stats[:, u, :], src_ps[:, u, :])
                own.link(last)
                alone(e, stood)
                for u in range(2):
                    last = v.bn_aggr(mv[:, u, :], stats[:, u, :])
                own.link(last)
                own.link(v.tensor_scalar(ln_ve[:, 0:2], mv[:, 0:2, 1], LN_EPS, None, ALU.add))
                v.reciprocal(ln_rc[:, 0:2], ln_ve[:, 0:2]).then_inc(var_sem, 1)

            def normed(dst_t, src_t, s):
                for u in range(2):
                    last = v.tensor_scalar(dst_t[:, u, :], src_t[:, u, :], mv[:, u, 0:1], ln_rs[:, u:u + 1],
                                           ALU.subtract, ALU.mult)
                last.then_inc(s, 1)

            own_m = 3 + 2 * NBATCH

            def m_body(i, s, j):
                g0 = KG * NSUP + MG * i
                before, spans = seg_values(e, mybir.EngineType.DVE, g0, MG, True)
                ch = own_m + 10 * i
                seg(g0, before, *spans[0])
                e.wait_ge(m_nd_ps, i + 1)
                own.at(ch)
                own.link(v.tensor_scalar(mden, bank(BC), ATT_EPS, 1.0 / N, ALU.add, ALU.mult))
                own.link(v.reciprocal(mden, mden))
                v.tensor_tensor(mmsg, bank(BB), mden, ALU.mult).then_inc(m_msg, 1)
                seg(g0 + 1, spans[0][1], *spans[1])
                e.wait_ge(m_y_ps, i + 1)
                norm_stats(bank(BC), m_v1, i, ch + 2)
                e.wait_ge(m_r1, i + 1)
                normed(myn, bank(BC), m_yn)
                seg(g0 + 2, spans[1][1], *spans[2])
                e.wait_ge(m_gr_ps, i + 1)
                if past(i, 2):
                    e.wait_ge(rg_out[s], 16 * j)
                v.tensor_tensor(mrg[s][:, :, D:2 * D], bank(BA), bcast(bl_s[:, :], 2), ALU.add).then_inc(m_gr, 1)
                seg(g0 + 3, spans[2][1], *spans[3])
                seg(g0 + 4, spans[3][1], *spans[4])
                seg(g0 + 5, spans[4][1], *spans[5])
                e.wait_ge(m_h2_ps, i + 1)
                norm_stats(bank(BF), m_v2, i, ch + 5)
                e.wait_ge(m_r2, i + 1)
                normed(mn2, bank(BF), m_n2)
                e.wait_ge(m_n2, i + 1)
                own.at(ch + 8)
                own.link(v.tensor_tensor(mn2, mn2, bcast(g2_s[:, :], 2), ALU.mult))
                own.link(v.tensor_tensor(mn2, mn2, bcast(b2_s[:, :], 2), ALU.add))
                e.wait_ge(m_xs, i + 1)
                v.tensor_tensor(mrg[s][:, :, 0:D], mn2, mrg[s][:, :, 0:D], ALU.add).then_inc(m_r, 1)
            steps(e, m_body, NSUP, 2)

            p = e.snap(pair)
            add_before(NBLK - 1, p)
            e.wait_ge(seg_added, p + 2)
            base = own_m + 10 * NSUP
            own.at(base)
            own.link(v.tensor_scalar(rcnt[:, :], agg[:, :, D], 1.0, None, ALU.max))
            own.link(v.reciprocal(rcnt[:, :], rcnt[:, :]))
            for s in range(2):
                e.wait_ge(rg_out[s], 16 * len(range(s, NSUP, 2)))

            own_g = base + 2

            def g_body(i, s, j):
                ch = own_g + 5 * i
                if past(i, 1):
                    e.wait_ge(g_T_ps, i)
                for u in range(2):
                    last = v.tensor_scalar(gma[:, u, :], agg[:, ds(2 * i + u, 1), 0:D], rcnt[:, ds(2 * i + u, 1)],
                                           None, ALU.mult)
                last.then_inc(g_ma, 1)
                e.wait_ge(g_in[s], 16 * j + 16)
                e.wait_ge(g_ps, i + 1)
                own.at(ch)
                own.link(v.tensor_tensor(gs, bank(BB), grg[s][:, :, D:2 * D], ALU.add))
                v.scalar_tensor_tensor(out=gx1, in0=gs, scalar=0.0, in1=grg[s][:, :, 0:D],
                                       op0=ALU.max, op1=ALU.add).then_inc(g_s, 1)
                e.wait_ge(g_s, i + 1)
                norm_stats(gx1, g_v, i, ch + 1)
                e.wait_ge(g_r, i + 1)
                if past(i, 2):
                    e.wait_ge(ff_out[s], 32 * j)
                normed(gff[s][:, :, 0:D], gx1, g_xn)
                e.wait_ge(g_xn, i + 1)
                v.tensor_tensor(gff[s][:, :, D:2 * D], gx1, gff[s][:, :, 0:D], ALU.add).then_inc(g_base, 1)
                for u in range(2):
                    last = v.tensor_tensor_reduce(out=gs[:, u, :], in0=gff[s][:, u, 0:D], in1=wr_s[:, :], scale=1.0,
                                                  scalar=0.0, op0=ALU.mult, op1=ALU.add,
                                                  accum_out=small[:, 44 + u:45 + u])
                last.then_inc(own_dve, 1)
                e.wait_ge(own_dve, ch + 5)
                v.tensor_scalar(wtok[:, ds(2 * i, 2)], small[:, 44:46], br_s[:, 0:1], None, ALU.add).then_inc(g_w, 1)
            steps(e, g_body, NSUP, 2)

            own.at(own_g + 5 * NSUP)
            e.wait_ge(g_w, NSUP)
            lastw = wtok[:, NBLK - 1:NBLK]
            own.link(v.tensor_scalar(small[:, 0:1], lastvalid[:, :], 1.0, 3.4e38, ALU.subtract, ALU.mult))
            own.link(v.tensor_tensor(lastw, lastw, lastvalid[:, :], ALU.mult))
            own.link(v.tensor_tensor(lastw, lastw, small[:, 0:1], ALU.add))
            own.link(v.memset(s_prefix, 0))
            own.link(v.memset(s_bit, -(1 << 31)))
            s0 = own_g + 5 * NSUP + own.n

            def key_bit(i, s, j):
                own.at(s0 + 7 * i)
                own.link(v.tensor_tensor(s_cand, s_prefix, s_bit, ALU.bitwise_or))
                own.link(v.tensor_scalar(s_m, s_cand, 31, -1, ALU.arith_shift_right, ALU.bitwise_xor))
                own.link(v.tensor_scalar(s_m, s_m, -(1 << 31), None, ALU.bitwise_or))
                own.link(v.tensor_tensor(s_f, s_m, s_cand, ALU.bitwise_xor))
                v.tensor_scalar(s_junk, wtok[:, :], s_f.bitcast(f32), None, ALU.is_ge, ALU.add,
                                accum_out=s_count).then_inc(s_cnt, 1)
                e.wait_ge(s_tot, i + 1)
                own.link(v.scalar_tensor_tensor(out=s_m, in0=ps[:, BA, 0:1], scalar=float(KK), in1=s_bit,
                                                op0=ALU.is_ge, op1=ALU.mult))
                own.link(v.tensor_tensor(s_prefix, s_prefix, s_m, ALU.bitwise_or))
                own.link(v.tensor_scalar(s_bit, s_bit, 1, None, ALU.logical_shift_right))
            steps(e, key_bit, 32, 2)
            own.at(s0 + 7 * 32)
            own.link(v.tensor_scalar(s_m, s_prefix, 31, -1, ALU.arith_shift_right, ALU.bitwise_xor))
            own.link(v.tensor_scalar(s_m, s_m, -(1 << 31), None, ALU.bitwise_or))
            own.link(v.tensor_tensor(s_f, s_m, s_prefix, ALU.bitwise_xor))
            thr = s_f.bitcast(f32)
            own.link(v.tensor_scalar(s_gt, wtok[:, :], thr, None, ALU.is_gt))
            own.link(v.tensor_reduce(s_count, s_gt, AX.X, ALU.add))
            v.tensor_scalar(s_eq, wtok[:, :], thr, None, ALU.is_equal).then_inc(s_cnt, 1)

            def ranks(n):
                e.wait_ge(s_tot, n)
                own.link(v.memset(s_sum[0][:, 0:1], 0.0))
                own.link(v.tensor_copy(s_sum[0][:, 1:NBLK], ps[:, BC, 0:NBLK - 1]))
                k, a = 1, 0
                while k < NBLK:
                    v.tensor_copy(s_sum[1 - a][:, 0:k], s_sum[a][:, 0:k])
                    own.link(v.tensor_tensor(s_sum[1 - a][:, k:NBLK], s_sum[a][:, k:NBLK],
                                             s_sum[a][:, 0:NBLK - k], ALU.add))
                    k, a = 2 * k, 1 - a
                own.link(v.tensor_tensor(s_rank, s_sum[a][:, 0:NBLK], ps[:, BB, 0:NBLK], ALU.add))

            ranks(33)
            own.link(v.tensor_scalar(small[:, 0:1], ps[:, BA, 0:1], -1.0, float(KK), ALU.mult, ALU.add))
            own.link(v.tensor_scalar(s_rank, s_rank, small[:, 0:1], None, ALU.is_lt))
            own.link(v.tensor_tensor(s_eq, s_eq, s_rank, ALU.mult))
            v.tensor_tensor(s_eq, s_eq, s_gt, ALU.add).then_inc(s_cnt, 1)
            ranks(34)
            own.link(v.tensor_copy(s_pos, s_rank))
            own.link(v.tensor_scalar(s_q, s_pos, 7, None, ALU.arith_shift_right))
            own.link(v.tensor_copy(s_colf, s_q))
            own.link(v.tensor_scalar(s_q, s_pos, P - 1, None, ALU.bitwise_and))
            own.link(v.tensor_copy(s_rank, s_q))
            own.link(v.scalar_tensor_tensor(out=s_rank, in0=s_rank, scalar=1.0, in1=s_eq, op0=ALU.add, op1=ALU.mult))
            own.link(v.tensor_scalar(s_rank, s_rank, 1.0, None, ALU.subtract))

            def place_block(c, s, j):
                if past(c, 3):
                    e.wait_ge(s_mm, c - 2)
                col = (lambda t: t[:, ds(c, 1)] if not isinstance(c, int) else t[:, c:c + 1])
                v.tensor_scalar(s_oh[s], iota16[:, :], col(s_rank), None, ALU.is_equal)
                v.tensor_scalar(s_pc[s][:, 0:NSEL], iotaf[:, 0:NSEL], col(s_colf), pcol[:, 0:1],
                                ALU.is_equal, ALU.mult)
                v.tensor_scalar(s_pc[s][:, NSEL:2 * NSEL], iotaf[:, 0:NSEL], col(s_colf), col(iotaf),
                                ALU.is_equal, ALU.mult).then_inc(s_a, 1)
            steps(e, place_block, NBLK, 3)
            e.wait_ge(s_mm, NBLK)
            own.link(v.tensor_scalar(s_sum[0][:, 0:NSEL], ps[:, BD, NSEL:2 * NSEL], float(P), None, ALU.mult))
            v.tensor_tensor(sel_idx, s_sum[0][:, 0:NSEL], ps[:, BD, 0:NSEL], ALU.add).then_inc(s_idx, 1)

            def f_body(i, s, j):
                n = 1 if isinstance(i, int) and i == NSEL // 2 else 2
                e.wait_ge(f_in[s], 32 * j + 16 * n)
                if past(i, 1):
                    e.wait_ge(f_o, i)
                for u in range(n):
                    last = v.tensor_tensor_reduce(out=f_junk[:, u, :], in0=frow[s][:, u, 0:D], in1=wr_s[:, :], scale=1.0,
                                                  scalar=0.0, op0=ALU.mult, op1=ALU.add,
                                                  accum_out=small[:, 44 + u:45 + u])
                last.then_inc(f_w, 1)
                e.wait_ge(f_w, 2 * i + 1)
                v.tensor_scalar(small[:, 46:46 + n], small[:, 44:44 + n], br_s[:, 0:1], None, ALU.add).then_inc(f_w, 1)
                e.wait_ge(f_y_ps, i + 1)
                v.tensor_tensor(f_junk[:, 0:n, :], bank(BF)[:, 0:n, :], bcast(fb2_s[:, :], n), ALU.add).then_inc(f_yb, 1)
                e.wait_ge(f_yb, i + 1)
                e.wait_ge(f_w, 2 * i + 2)
                if past(i, 2):
                    e.wait_ge(f_out[s], 32 * j)
                for u in range(n):
                    last = v.scalar_tensor_tensor(out=fo[s][:, u, :], in0=f_junk[:, u, :], scalar=small[:, 46 + u:47 + u],
                                                  in1=frow[s][:, u, D:2 * D], op0=ALU.mult, op1=ALU.add)
                last.then_inc(f_o, 1)
            steps(e, f_body, NSEL // 2 + 1, 2, 2)

        @block.scalar
        def _(e):
            a = nc.scalar
            e.dma_start(wlr_n[:, 0:2, :], W_l.rearrange("(c p) n -> p c n", p=P)).then_inc(wlr_in, 16)
            e.dma_start(wlr_n[:, 2:4, :], W_r.rearrange("(c p) n -> p c n", p=P)).then_inc(wlr_in, 16)
            loads = [(wq_s[:, :, :], Wq.rearrange("(k p) n -> p k n", p=P)),
                     (wkv_s[:, :, 0:D], Wk.rearrange("(k p) n -> p k n", p=P)),
                     (wkv_s[:, :, D:2 * D], Wv.rearrange("(k p) n -> p k n", p=P)),
                     (wm_s[:, :, :], Wm.rearrange("(k p) n -> p k n", p=P)),
                     (w1_s[:, :, :], W1.rearrange("(k p) n -> p k n", p=P)),
                     (w2_s[:, :, :], W2.rearrange("(k p) n -> p k n", p=P)),
                     (bl_s[:, :], b_l.unsqueeze(0).to_broadcast([P, D])),
                     (g2_s[:, :], g2.unsqueeze(0).to_broadcast([P, D])),
                     (b2_s[:, :], b2.unsqueeze(0).to_broadcast([P, D])),
                     (fb2_s[:, :], fb2.unsqueeze(0).to_broadcast([P, D])),
                     (wr_s[:, :], wr.rearrange("d o -> o d").to_broadcast([P, D])),
                     (br_s[:, :], br.unsqueeze(0).to_broadcast([P, 1])),
                     (g1_s[:, :], g1.rearrange("(c p) -> p c", p=P)),
                     (b1_s[:, :], b1.rearrange("(c p) -> p c", p=P)),
                     (fb1_s[:, :], fb1.rearrange("(c p) -> p c", p=P))]
            with nc.allow_non_contiguous_dma("a few hundred biases"):
                for to, of in loads:
                    e.dma_start(to, of).then_inc(wts_in, 16)

            for c in range(CH):
                n = min(P, NG - c * P)
                e.wait_ge(tr_ps, c + 1)
                a.activation(srcI[:, c * P:c * P + n, :],
                             bank(c % 8, (TPG, P)).rearrange("p t g -> p g t")[:, 0:n, :], ACT.Copy).then_inc(tr_ev, 1)

            def ln_norm(m, s, j):
                e.wait_ge(ln_var, 2 * m + 2)
                a.activation(ln_rs, ln_rc, ACT.Sqrt).then_inc(ln_rstd, 1)
                e.wait_ge(ln_nmr, m + 1)
                e.wait_ge(ln_rstd, m + 1)
                if past(m, 1):
                    e.wait_ge(ln_hi, m)
                    e.wait_ge(ln_lo, m)
                for k in range(BPB):
                    last = a.activation(ln_n[:, k, :], ln_x[s][:, k, :], ACT.Identity,
                                        bias=ln_nm[:, k:k + 1], scale=ln_rs[:, k:k + 1])
                last.then_inc(ln_xn, 1)
            steps(e, ln_norm, NBATCH, 2)

            def xn_of(to, of, i, done):
                for u in range(2):
                    k = 2 * i + u
                    c = slice(k, k + 1) if isinstance(k, int) else ds(k, 1)
                    last = a.activation(to[:, u, :], of[:, u, :], ACT.Identity, bias=nmr[:, c], scale=rstd[:, c])
                last.then_inc(done, 1)

            e.wait_ge(ln_tab, NBATCH)
            e.wait_ge(k_x_in[0], 16)
            xn_of(kxn, kx[0], 0, k_xn)
            e.wait_ge(k_xT_ps, 1)
            a.activation(kxT[0], bank(BA), ACT.Copy).then_inc(k_xnT, 1)

            def k_body(i, s, j):
                more = not (isinstance(i, int) and i == NSUP - 1)
                s1 = (s + 1) % 3
                if more:
                    e.wait_ge(k_x_in[s1], 16 * (j + (s + 1) // 3) + 16)
                    e.wait_ge(k_xT_ps, i + 1)
                    xn_of(kxn, kx[s1], i + 1, k_xn)
                e.wait_ge(k_kmin, i + 1)
                a.activation(kmin, kmin, ACT.Exp).then_inc(k_kexp, 1)
                if past(i, 1):
                    e.wait_ge(k_acc, i)
                e.wait_ge(k_ones, 1)
                for u in range(2):
                    last = a.activation(vaug[:, u, :, 0:P], bank(BD)[:, u, :].rearrange("p (c n) -> p c n", c=2),
                                        ACT.Copy)
                if not more:
                    for c in range(2):
                        last = a.activation(vaug[:, 1, c, P:P + 1], lastvalid[:, :], ACT.Copy)
                last.then_inc(k_v, 1)
                e.wait_ge(k_qmin, i + 1)
                a.activation(qmin, qmin, ACT.Exp).then_inc(k_qexp, 1)
                if more:
                    e.wait_ge(k_xT_ps, i + 2)
                    if past(i, 2):
                        e.wait_ge(k_q_ps, i - 1)
                    a.activation(kxT[s1], bank(BA), ACT.Copy).then_inc(k_xnT, 1)
            steps(e, k_body, NSUP, 3)

            e.wait_ge(m_x_in[0], 16)
            xn_of(mxn, mx[0], 0, m_xn)

            def m_body(i, s, j):
                more = not (isinstance(i, int) and i == NSUP - 1)
                e.wait_ge(m_xT_ps, i + 1)
                if past(i, 2):
                    e.wait_ge(m_h1_ps, 2 * i - 2)
                a.activation(mxT[s], bank(BA), ACT.Copy).then_inc(m_xnT, 1)
                if past(i, 2):
                    e.wait_ge(rg_out[s], 16 * j)
                for u in range(2):
                    k = 2 * i + u
                    c = slice(k, k + 1) if isinstance(k, int) else ds(k, 1)
                    last = a.activation(mrg[s][:, u, 0:D], mx[s][:, u, :], ACT.Identity, bias=res_b[:, c], scale=res_s[:, c])
                last.then_inc(m_xs, 1)
                e.wait_ge(m_v1, i + 1)
                a.activation(ln_rs[:, 0:2], ln_rc[:, 0:2], ACT.Sqrt).then_inc(m_r1, 1)
                e.wait_ge(m_yT_ps, i + 1)
                for c in range(2):
                    last = a.activation(mynT[:, c, :], bank(BB)[:, c, :], ACT.Identity,
                                        bias=b1_s[:, c:c + 1], scale=g1_s[:, c:c + 1])
                last.then_inc(m_ynT, 1)
                for h in range(2):
                    e.wait_ge(m_h1_ps, 2 * i + h + 1)
                    if past(i, 1):
                        e.wait_ge(m_h2_ps, i)
                    a.activation(mh1[:, 2 * h:2 * h + 2, :], bank(BD + h), ACT.Relu).then_inc(m_h1, 1)
                if more:
                    e.wait_ge(m_x_in[1 - s], 16 * (j + s) + 16)
                    xn_of(mxn, mx[1 - s], i + 1, m_xn)
                e.wait_ge(m_v2, i + 1)
                a.activation(ln_rs[:, 0:2], ln_rc[:, 0:2], ACT.Sqrt).then_inc(m_r2, 1)
            steps(e, m_body, NSUP, 2)

            def g_body(i, s, j):
                e.wait_ge(g_T_ps, i + 1)
                if past(i, 1):
                    e.wait_ge(g_ps, i)
                a.activation(gaT, bank(BA), ACT.Copy).then_inc(g_aT, 1)
                e.wait_ge(g_v, i + 1)
                a.activation(ln_rs[:, 0:2], ln_rc[:, 0:2], ACT.Sqrt).then_inc(g_r, 1)
            steps(e, g_body, NSUP, 2)

            def f_copy(i, s):
                e.wait_ge(f_T_ps, i + 1)
                if past(i, 2):
                    e.wait_ge(f_h_ps, 4 * (i - 1))
                a.activation(f_xTs[s], bank(BA), ACT.Copy).then_inc(f_xT, 1)

            f_copy(0, 0)

            def f_body(i, s, j):
                for h in range(4):
                    e.wait_ge(f_h_ps, 4 * i + h + 1)
                    if past(i, 1):
                        e.wait_ge(f_y_ps, i)
                    for c in (2 * h, 2 * h + 1):
                        last = a.activation(fh[:, c, :], bank(BB + h)[:, c % 2, :], ACT.Gelu_apprx_tanh,
                                            bias=fb1_s[:, c:c + 1])
                    last.then_inc(f_h, 1)
                    if h == 1 and not (isinstance(i, int) and i == NSEL // 2):
                        f_copy(i + 1, 1 - s)
            steps(e, f_body, NSEL // 2 + 1, 2, 2)

        @block.tensor
        def _(e):
            t = nc.tensor
            pair = e.alloc_register("pe_pair")
            e.reg_mov(pair, 0)

            e.wait_ge(cst, 3)
            e.wait_ge(edges_cast, 2)
            for k in range(2 * CH):
                for q in range(TPG):
                    last = t.transpose(bank(k % 8, (TPG, P))[:, q, :], edges_f[:, k // CH, k % CH, q * P:(q + 1) * P],
                                       ident[:, :])
                last.then_inc(tr_ps, 1)
            e.wait_ge(wlr_in, 32)
            e.wait_ge(tr_ev, 2 * CH)
            for k in range(2):
                for i_ in range(2):
                    for o_ in range(2):
                        last = t.transpose(bank(k)[:, i_, o_ * P:(o_ + 1) * P],
                                           wlr_n[:, 2 * k + o_, i_ * P:(i_ + 1) * P], ident[:, :])
                last.then_inc(tr_ps, 1)
            e.wait_ge(wts_in, 16 * 15)
            e.wait_ge(tr_ev, 2 * CH + 2)

            def transposes(b, of):
                for u in range(2):
                    for c in range(2):
                        last = t.transpose(bank(b)[:, c, u * P:(u + 1) * P], of[:, u, c * P:(c + 1) * P], ident[:, :])
                return last

            def seg(slot, use, first, last_b):
                with e.Fori(first, last_b + 1):
                    p = e.snap(pair)
                    e.wait_ge(rows_in[slot], 16 * TPG * use + 16 * TPG)
                    e.wait_ge(oh_ready, p + 1)
                    e.wait_ge(seg_added, p + 1)
                    for q in range(TPG):
                        oh = onehot[:, ds(p % 2, 1), q, :]
                        k = TPG * slot + q
                        t.matmul(ps[:, ds(BG + p % 2, 1), 0:D], oh, gath[:, k, 0:D], start=q == 0, stop=False,
                                 skip_group_check=True)
                        last = t.matmul(ps[:, ds(BG + p % 2, 1), 0:AGW], oh, gath[:, k, D:2 * D + 1], start=False,
                                        stop=q == TPG - 1, skip_group_check=True)
                    last.then_inc(seg_done, 1)
                    e.reg_add(pair, pair, 1)

            e.wait_ge(bnd_in, 16)
            e.wait_ge(ones_set, 1)
            e.wait_ge(agg_zero, NBLK // 14)
            t.matmul(ps[:, BE, 0:2 * (P + 1)], agg[:, 0, 0:P], agg[:, 1:3, 0:P + 1], start=True, stop=False,
                     skip_group_check=True)

            e.wait_ge(k_xn, 1)
            transposes(BA, kxn).then_inc(k_xT_ps, 1)

            def k_body(i, s, j):
                more = not (isinstance(i, int) and i == NSUP - 1)
                _, spans = seg_values(e, mybir.EngineType.PE, KG * i, KG, False)
                e.wait_ge(k_xnT, i + 1)
                if past(i, 1):
                    e.wait_ge(k_K, i)
                    e.wait_ge(k_v, i)
                for u in range(2):
                    for b in range(2):
                        for c in range(2):
                            last = t.matmul(bank(BC + b)[:, u, :], kxT[s][:, c, u * P:(u + 1) * P],
                                            wkv_s[:, c, b * D:(b + 1) * D], start=c == 0, stop=c == 1)
                last.then_inc(k_kv_ps, 1)
                if more:
                    e.wait_ge(k_xn, i + 2)
                    transposes(BA, kxn).then_inc(k_xT_ps, 1)
                if past(i, 1):
                    e.wait_ge(k_Q, i)
                for o_ in range(2):
                    for c in range(2):
                        last = t.matmul(bank(BB)[:, o_, :], wq_s[:, c, o_ * P:(o_ + 1) * P], kxT[s][:, c, :],
                                        start=c == 0, stop=c == 1)
                last.then_inc(k_q_ps, 1)
                for g in range(KG):
                    seg(*k_place(s, j, g), *spans[g])
                e.wait_ge(k_K, i + 1)
                e.wait_ge(k_v, i + 1)
                for u in range(2):
                    for c in range(2):
                        end = not more and u == 1 and c == 1
                        last = t.matmul(ps[:, BE, c * (P + 1):(c + 1) * (P + 1)], kk_s[:, u, c * P:(c + 1) * P],
                                        vaug[:, u, c, :], start=False, stop=end, skip_group_check=True)
                last.then_inc(k_acc, 1)
            steps(e, k_body, NSUP, 3)

            e.wait_ge(kvbd_set, 2)

            def m_body(i, s, j):
                _, spans = seg_values(e, mybir.EngineType.PE, KG * NSUP + MG * i, MG, False)
                e.wait_ge(m_q_in[s], 16 * j + 16)
                if past(i, 1):
                    e.wait_ge(m_ynT, i)
                    e.wait_ge(m_yn, i)
                for b, w in ((BB, kvbd), (BC, ksbd)):
                    for c in range(2):
                        last = t.matmul(bank(b)[:, c, :], w[:, c, :], mq[s][:, c, :], start=True, stop=True)
                last.then_inc(m_nd_ps, 1)
                e.wait_ge(m_xn, i + 1)
                if past(i, 1):
                    e.wait_ge(m_gr, i)
                transposes(BA, mxn).then_inc(m_xT_ps, 1)
                seg(*m_place(i, 0), *spans[0])
                e.wait_ge(m_msg, i + 1)
                for u in range(2):
                    for c in range(2):
                        last = t.matmul(bank(BC)[:, u, :], mmsg[:, c, u * P:(u + 1) * P], wm_s[:, c, :],
                                        start=c == 0, stop=c == 1)
                last.then_inc(m_y_ps, 1)
                seg(*m_place(i, 1), *spans[1])
                e.wait_ge(m_xnT, i + 1)
                for u in range(2):
                    for c in range(2):
                        last = t.matmul(bank(BA)[:, u, :], mxT[s][:, c, u * P:(u + 1) * P], wrT[:, c, :],
                                        start=c == 0, stop=c == 1)
                last.then_inc(m_gr_ps, 1)
                seg(*m_place(i, 2), *spans[2])
                e.wait_ge(m_yn, i + 1)
                transposes(BB, myn).then_inc(m_yT_ps, 1)
                if past(i, 1):
                    e.wait_ge(m_h1, 2 * i)
                for o_ in range(4):
                    for c in range(4):
                        if o_ == 0 and c == 2:
                            e.wait_ge(m_ynT, i + 1)
                        last = t.matmul(bank(BD + o_ // 2)[:, o_ % 2, :], w1_s[:, c, o_ * P:(o_ + 1) * P],
                                        (mxT[s] if c < 2 else mynT)[:, c % 2, :], start=c == 0, stop=c == 3)
                    if o_ % 2:
                        last.then_inc(m_h1_ps, 1)
                seg(*m_place(i, 3), *spans[3])
                e.wait_ge(m_h1, 2 * i + 2)
                if past(i, 1):
                    e.wait_ge(m_n2, i)
                for u in range(2):
                    for c in range(4):
                        last = t.matmul(bank(BF)[:, u, :], mh1[:, c, u * P:(u + 1) * P], w2_s[:, c, :],
                                        start=c == 0, stop=c == 3)
                last.then_inc(m_h2_ps, 1)
                seg(*m_place(i, 4), *spans[4])
                seg(*m_place(i, 5), *spans[5])
            steps(e, m_body, NSUP, 2)

            def g_body(i, s, j):
                e.wait_ge(g_ma, i + 1)
                transposes(BA, gma).then_inc(g_T_ps, 1)
                e.wait_ge(g_aT, i + 1)
                if past(i, 1):
                    e.wait_ge(g_s, i)
                for u in range(2):
                    for c in range(2):
                        last = t.matmul(bank(BB)[:, u, :], gaT[:, c, u * P:(u + 1) * P], wlT[:, c, :],
                                        start=c == 0, stop=c == 1)
                last.then_inc(g_ps, 1)
            steps(e, g_body, NSUP, 2)

            def total(i, s, j):
                e.wait_ge(s_cnt, i + 1)
                t.matmul(ps[:, BA, 0:1], ones[:, :], s_count, start=True, stop=True).then_inc(s_tot, 1)
            steps(e, total, 32, 2)
            for n, marks in ((32, s_eq), (33, s_eq)):
                e.wait_ge(s_cnt, n + 1)
                if n == 32:
                    t.matmul(ps[:, BA, 0:1], ones[:, :], s_count, start=True, stop=True)
                t.matmul(ps[:, BB, 0:NBLK], tri[:, :], marks, start=True, stop=True)
                t.matmul(ps[:, BC, 0:NBLK], ones[:, :], marks, start=True, stop=True).then_inc(s_tot, 1)

            def place_block(c, s, j):
                e.wait_ge(s_a, c + 1)
                t.matmul(ps[:, BD, 0:2 * NSEL], s_oh[s], s_pc[s], start=isinstance(c, int) and c == 0,
                         stop=isinstance(c, int) and c == NBLK - 1, skip_group_check=True).then_inc(s_mm, 1)
            steps(e, place_block, NBLK, 3)

            e.wait_ge(ffw_in, 32)

            def f_T(i, s, j, n):
                e.wait_ge(f_in[s], 32 * j + 16 * n)
                if past(i, 1):
                    e.wait_ge(f_xT, i)
                for u in range(n):
                    for c in range(2):
                        last = t.transpose(bank(BA)[:, c, u * P:(u + 1) * P], frow[s][:, u, c * P:(c + 1) * P],
                                           ident[:, :])
                last.then_inc(f_T_ps, 1)
            f_T(0, 0, 0, 2)

            def f_body(i, s, j):
                end = isinstance(i, int) and i == NSEL // 2
                n = 1 if end else 2
                e.wait_ge(f_xT, i + 1)
                if past(i, 1):
                    e.wait_ge(f_h, 4 * i)
                for o_ in range(HF // P):
                    for c in range(2):
                        last = t.matmul(bank(BB + o_ // 2)[:, o_ % 2, :], fw1_s[:, c, o_ * P:(o_ + 1) * P],
                                        f_xTs[s][:, c, :], start=c == 0, stop=c == 1)
                    if o_ % 2:
                        last.then_inc(f_h_ps, 1)
                if not end:
                    k = 1 if isinstance(i, int) and i == NSEL // 2 - 1 else 2
                    f_T(i + 1, 1 - s, j + s, k)
                e.wait_ge(f_h, 4 * i + 4)
                if past(i, 1):
                    e.wait_ge(f_yb, i)
                for u in range(n):
                    for c in range(HF // P):
                        last = t.matmul(bank(BF)[:, u, :], fh[:, c, u * P:(u + 1) * P], fw2_s[:, c, :],
                                        start=c == 0, stop=c == HF // P - 1)
                last.then_inc(f_y_ps, 1)
            steps(e, f_body, NSEL // 2 + 1, 2, 2)


_INS = {"x": "x", "src": "src", "dst": "dst", "W_l": "L0_gnn_W_l", "b_l": "L0_gnn_b_l", "W_r": "L0_gnn_W_r",
        "Wq": "L0_mix_Wq", "Wk": "L0_mix_Wk", "Wv": "L0_mix_Wv", "Wm": "L0_mix_Wm", "W1": "L0_mix_W1",
        "W2": "L0_mix_W2", "g1": "L0_mix_g1", "b1": "L0_mix_b1", "g2": "L0_mix_g2", "b2": "L0_mix_b2",
        "wr": "L0_ffn_wr", "br": "L0_ffn_br", "w1": "L0_ffn_w1", "fb1": "L0_ffn_b1", "w2": "L0_ffn_w2",
        "fb2": "L0_ffn_b2"}


def kernel(**inputs):
    import concourse.bacc as bacc
    from concourse.bass_utils import run_bass_kernel_spmd

    nc = bacc.Bacc("TRN2", target_bir_lowering=False, num_devices=1)
    arrays, args = {}, {}
    for name, key in _INS.items():
        a = np.ascontiguousarray(inputs[key])
        if name == "x":
            padded = np.zeros((NPAD, D), a.dtype)
            padded[:N] = a
            a = padded
        arrays[f"{name}_in"] = a
        args[name] = nc.dram_tensor(f"{name}_in", a.shape, mybir.dt.from_np(a.dtype), kind="ExternalInput").ap()
    args["out"] = nc.dram_tensor("out_rows", (NPAD, D), f32, kind="ExternalOutput").ap()
    build(nc, **args)
    r = run_bass_kernel_spmd(nc, [arrays], core_ids=[0])
    return r.results[0]["out_rows"][:N]
```

```python
import numpy as np
import concourse.bass as bass
from concourse import mybir
from contextlib import ExitStack

f32 = mybir.dt.float32
f16 = mybir.dt.float16
f32r = mybir.dt.float32r
i32 = mybir.dt.int32
ALU = mybir.AluOpType
ACT = mybir.ActivationFunctionType
AX = mybir.AxisListType

P = 128
N, D, E = 12500, 256, 200000
NBLK = -(-N // P)
NPAD = NBLK * P
LASTROWS = N - (NBLK - 1) * P
NSUP = NBLK // 2
SB = 2 * P
TPG = 4
GE = TPG * P
KG, MG = 2, 6
NG = NSUP * (KG + MG)
RING = 6
FULLG, RESTE = E // GE, E % GE
CH = -(-NG // P)
LASTC = FULLG - (CH - 1) * P
PADNODE = NPAD - 1
HEADS = 8
DH = D // HEADS
HPC = P // DH
LN_EPS, ATT_EPS = 1e-5, 1e-6
HF = 4 * D
KK = max(1, N // 2) - 1
NSEL = -(-KK // P)
LASTSEL = KK - (NSEL - 1) * P
DIGIT = 4
NDIG = 32 // DIGIT
CAND = (1 << DIGIT) - 1
FSTEPS = -(-NSEL // 2)
FSLOTS = 3
BPB = 7
NBATCH = NBLK // BPB
GROW = 2 * D + 4
AGW = D + 1

assert NBLK % 2 == 0 and NSEL % 2 == 1 and NBLK % BPB == 0 and NG * GE >= E and NG <= CH * P
assert 0 < LASTC < P and KG * 3 == RING and MG == RING


def past(i, k):
    return not isinstance(i, int) or i >= k


def steps(eng, body, n, unroll, tail=0):
    for i in range(min(unroll, n)):
        body(i, i, 0)
    end = (n - tail) // unroll
    if end > 1:
        with eng.Fori(1, end) as j:
            for s in range(unroll):
                body(j * unroll + s, s, j)
    for i in range(max(end, 1) * unroll, n):
        body(i, i % unroll, i // unroll)


def alone(eng, stood):
    eng.sem_inc(stood, 1)


class Chain:

    def __init__(self, eng, sem):
        self.eng, self.sem, self.base, self.n = eng, sem, 0, 0

    def at(self, base):
        self.base, self.n = base, 0

    def link(self, ins):
        self.n += 1
        ins.then_inc(self.sem, 1)
        self.eng.wait_ge(self.sem, self.base + self.n)


def build(nc, x, src, dst, W_l, b_l, W_r, Wq, Wk, Wv, Wm, W1, W2, g1, b1, g2, b2, wr, br, w1, fb1, w2, fb2, out):
    ds = bass.ds
    ctx = ExitStack()
    with ctx:
        def sb(name, shape, dt=f32):
            return ctx.enter_context(nc.sbuf_tensor(name, shape, dt))

        def sem(name):
            return ctx.enter_context(nc.semaphore(name))

        xtab = nc.dram_tensor("xtab", (NPAD, 2 * D), f16, kind="Internal").ap()
        bounds_d = nc.dram_tensor("bounds_d", (CH * P, 2), i32, kind="Internal").ap()
        q_d = nc.dram_tensor("q_d", (NSUP, P, 2 * SB), f32, kind="Internal").ap()
        xt_d = nc.dram_tensor("xt_d", (NSUP, P, 2 * SB), f32, kind="Internal").ap()
        r_d = nc.dram_tensor("r_d", (NPAD, D), f32, kind="Internal").ap()
        ff_d = nc.dram_tensor("ff_d", (NPAD, 2 * D), f32, kind="Internal").ap()

        def rows(t, i, n=2):
            return t.rearrange("(b p) c -> p b c", p=P)[:, ds(i, n) if not isinstance(i, int) else slice(i, i + n), :]

        def turned(t, i):
            return t[ds(i, 1) if not isinstance(i, int) else slice(i, i + 1), :, :].rearrange("o p c -> p (o c)")

        def flat(v):
            return v.rearrange("p a b -> p (a b)")

        with nc.sbuf_tensor("agg", [P, NBLK, AGW], f32) as agg:
            pass
        split_raw = sb("split_raw", [P, NBLK, AGW], f32r)
        gath_raw = sb("gath_raw", [P, RING * TPG * GROW // 2])
        gath = gath_raw[:, :].bitcast(f16).rearrange("p (s c) -> p s c", c=GROW)
        edges_i = gath_raw[:, 0:2 * CH * GE].bitcast(i32).rearrange("p (a c e) -> p a c e", a=2, c=CH)
        edges_f = gath_raw[:, 0:2 * CH * GE].rearrange("p (a c e) -> p a c e", a=2, c=CH)
        wq_s = sb("wq_s", [P, 2, D])
        wkv_s = sb("wkv_s", [P, 2, 2 * D])
        wm_s = sb("wm_s", [P, 2, D])
        w1_s = sb("w1_s", [P, 4, 2 * D])
        w2_s = sb("w2_s", [P, 4, D])
        wlr_n = gath_raw[:, 2 * CH * GE:2 * CH * GE + 4 * D].rearrange("p (a n) -> p a n", n=D)
        wlT = sb("wlT", [P, 2, D])
        wrT = sb("wrT", [P, 2, D])
        dstF = sb("dstF", [P, NG, TPG])
        srcI = sb("srcI", [P, NG, TPG], i32)
        rstd = sb("rstd", [P, NBLK])
        nmr = sb("nmr", [P, NBLK])
        res_s = sb("res_s", [P, NBLK])
        res_b = sb("res_b", [P, NBLK])
        wtok = sb("wtok", [P, NBLK])
        bl_s = sb("bl_s", [P, D])
        g2_s = sb("g2_s", [P, D])
        b2_s = sb("b2_s", [P, D])
        fb2_s = sb("fb2_s", [P, D])
        wr_s = sb("wr_s", [P, D])
        br_s = sb("br_s", [P, 1])
        g1_s = sb("g1_s", [P, 2])
        b1_s = sb("b1_s", [P, 2])
        fb1_s = sb("fb1_s", [P, HF // P])
        ident = sb("ident", [P, P])
        ones = sb("ones", [P, P])
        tri = sb("tri", [P, P])
        headm = sb("headm", [P, P])
        iota16 = sb("iota16", [P, P], f16)
        iotaf = sb("iotaf", [P, P])
        blkbase = sb("blkbase", [P, NBLK])
        pcol = sb("pcol", [P, 1])
        lastvalid = sb("lastvalid", [P, 1])
        onehot = sb("onehot", [P, 2, TPG, P], f16)
        stage = sb("stage", [P, 2, RING, TPG], i32)
        bnd = sb("bnd", [1, 2 * NG], i32)
        kvbd = sb("kvbd", [P, 2, P])
        kshd = sb("kshd", [P, 2, HPC])
        mden = sb("mden", [P, 2 * HEADS])
        rcnt = sb("rcnt", [P, NBLK])
        small_i = sb("small_i", [P, 2 * CH], i32)
        stats = sb("stats", [P, BPB, 6])
        mv = sb("mv", [P, BPB, 2])
        small = sb("small", [P, 64])
        work = sb("work", [P, 7680])

        def part(base, a, shape):
            n = int(np.prod(shape))
            v = base[:, a:a + n]
            if len(shape) == 2:
                v = v.rearrange("p (a b) -> p a b", a=shape[0])
            if len(shape) == 3:
                v = v.rearrange("p (a b c) -> p a b c", a=shape[0], b=shape[1])
            return v

        ps = ctx.enter_context(nc.psum_tensor("ps", [P, 8, 512], f32))
        BA, BB, BC, BD, BE, BF, BG = range(7)

        G_T = (BA, BD)

        def bank(b, shape=(2, 256)):
            return part(ps[:, b, :], 0, shape)

        cst = sem("cst")
        stood = sem("stood")
        wts_in = sem("wts_in")
        wlr_in = sem("wlr_in")
        ffw_in = sem("ffw_in")
        edges_in = sem("edges_in")
        edges_pad = sem("edges_pad")
        edges_cast = sem("edges_cast")
        tr_ps = sem("tr_ps")
        tr_ev = sem("tr_ev")
        bnd_out = sem("bnd_out")
        bnd_in = sem("bnd_in")
        bnd_ready = sem("bnd_ready")
        agg_zero = sem("agg_zero")
        ln_x_in = [sem(f"ln_x_in{i}") for i in range(4)]
        ln_xn = sem("ln_xn")
        ln_var = sem("ln_var")
        ln_rstd = sem("ln_rstd")
        ln_hi = sem("ln_hi")
        ln_lo = sem("ln_lo")
        ln_tab = sem("ln_tab")
        res_set = sem("res_set")
        ln_out = [sem(f"ln_out{i}") for i in range(2)]
        own_dve = sem("own_dve")
        own_act = sem("own_act")
        oh_ready = sem("oh_ready")
        seg_done = sem("seg_done")
        seg_added = sem("seg_added")
        grp_used = sem("grp_used")
        rows_in = [sem(f"rows_in{i}") for i in range(RING)]
        ones_set = sem("ones_set")
        stage_set = sem("stage_set")
        k_x_in = [sem(f"k_x_in{i}") for i in range(3)]
        k_xn = sem("k_xn")
        k_xT_ps = sem("k_xT_ps")
        k_xnT = sem("k_xnT")
        k_kv_ps = sem("k_kv_ps")
        k_q_ps = sem("k_q_ps")
        k_kmin = sem("k_kmin")
        k_qmin = sem("k_qmin")
        k_kexp = sem("k_kexp")
        k_qexp = sem("k_qexp")
        k_v = sem("k_v")
        k_K = sem("k_K")
        k_Q = sem("k_Q")
        k_acc = sem("k_acc")
        k_ones = sem("k_ones")
        xt_out = [sem(f"xt_out{i}") for i in range(3)]
        q_out = [sem(f"q_out{i}") for i in range(3)]
        kvbd_set = sem("kvbd_set")
        m_x_in = [sem(f"m_x_in{i}") for i in range(2)]
        m_xT_in = [sem(f"m_xT_in{i}") for i in range(2)]
        m_q_in = [sem(f"m_q_in{i}") for i in range(2)]
        m_xs = sem("m_xs")
        m_nd_ps = sem("m_nd_ps")
        m_msg = sem("m_msg")
        m_msgT_ps = sem("m_msgT_ps")
        m_msgT = sem("m_msgT")
        m_y_ps = sem("m_y_ps")
        m_v1 = sem("m_v1")
        m_yn = sem("m_yn")
        m_yT_ps = sem("m_yT_ps")
        m_ynT = sem("m_ynT")
        m_h1_ps = sem("m_h1_ps")
        m_h1 = sem("m_h1")
        m_h2_ps = sem("m_h2_ps")
        m_v2 = sem("m_v2")
        m_n2 = sem("m_n2")
        m_r = sem("m_r")
        r_out = [sem(f"r_out{i}") for i in range(2)]
        agg_done = sem("agg_done")
        g_in = [sem(f"g_in{i}") for i in range(4)]
        g_ma = sem("g_ma")
        g_T_ps = sem("g_T_ps")
        g_aT = sem("g_aT")
        g_ps = sem("g_ps")
        g_s = sem("g_s")
        g_v = sem("g_v")
        g_base = sem("g_base")
        g_w = sem("g_w")
        ff_out = [sem(f"ff_out{i}") for i in range(2)]
        s_cnt = sem("s_cnt")
        s_tot = sem("s_tot")
        s_a = sem("s_a")
        s_mm = sem("s_mm")
        s_idx = sem("s_idx")
        fstage = [sem(f"fstage{i}") for i in range(FSLOTS)]
        f_in = [sem(f"f_in{i}") for i in range(FSLOTS)]
        f_T_ps = sem("f_T_ps")
        f_wh = sem("f_wh")
        f_wl = sem("f_wl")
        f_xT_h = sem("f_xT_h")
        f_xT = sem("f_xT")
        f_g = sem("f_g")
        f_hh = sem("f_hh")
        f_h_ps = sem("f_h_ps")
        f_h = sem("f_h")
        f_y_ps = sem("f_y_ps")
        f_w = sem("f_w")
        f_yb = sem("f_yb")
        f_o = sem("f_o")
        f_out = [sem(f"f_out{i}") for i in range(FSLOTS)]

        ln_x = [part(work, s * BPB * D, (BPB, D)) for s in range(4)]
        ln_t = [gath_raw[:, s * BPB * D:(s + 1) * BPB * D].bitcast(f16).rearrange("p (b c) -> p b c", c=2 * D)
                for s in range(2)]
        ln_ve, ln_rc = (small[:, a:a + BPB] for a in (32, 56))
        ln_st, ln_mv = ([t[:, 2 * k:2 * k + 2, :] for k in range(2)] for t in (stats, mv))
        ln_ng, ln_v2, ln_c2, ln_f2, ln_b2, ln_g2 = ([small[:, a + 2 * k:a + 2 * k + 2] for k in range(2)]
                                                    for a in (4, 0, 8, 16, 24, 48))
        kx = [part(work, 512 * s, (2, D)) for s in range(3)]
        kxn = part(work, 1536, (2, D))
        kxT = [part(work, 2048 + 512 * s, (2, SB)) for s in range(3)]
        kmin = part(work, 3584, (2, D))
        kk_s = part(work, 4096, (2, D))
        vaug = part(work, 4608, (2, 2, P + 1))
        qmin = part(work, 5136, (2, SB))
        qout = [part(work, 5648 + 512 * s, (2, SB)) for s in range(3)]
        mx = [part(work, 512 * s, (2, D)) for s in range(2)]
        mxT = [part(work, 1024 + 512 * s, (2, SB)) for s in range(2)]
        mq = [part(work, 2048 + 512 * s, (2, SB)) for s in range(2)]
        mmsgT = part(work, 3072, (2, SB))
        mynT = part(work, 3584, (2, SB))
        mmsg = myn = part(work, 4096, (2, D))
        mh1 = part(work, 4608, (4, SB))
        mn2 = part(work, 6656, (2, D))
        mr = [part(work, 5632 + 512 * s, (2, D)) for s in range(2)]
        gr = [part(work, 512 * s, (2, D)) for s in range(4)]
        gxT = [w1_s[:, s, :].rearrange("p (a b) -> p a b", a=2) for s in range(4)]
        gma = [part(work, 2048 + 512 * s, (2, D)) for s in range(2)]
        gaT = [part(work, 3072 + 512 * s, (2, SB)) for s in range(2)]
        gx1 = [part(work, 4096 + 512 * s, (2, D)) for s in range(2)]
        gff = [part(work, 5120 + 1024 * s, (2, 2 * D)) for s in range(2)]
        gs = part(work, 7168, (2, D))
        pool2 = agg[:, :, :].rearrange("p b c -> p (b c)")
        pool2r = split_raw[:, :, :].rearrange("p b c -> p (b c)")
        s_gt, s_eq, s_rank, s_colf = (pool2[:, 128 * k:128 * k + NBLK] for k in range(4))
        s_pos, s_q = (pool2[:, 128 * k:128 * k + NBLK].bitcast(i32) for k in (5, 6))
        s_sum = [pool2[:, 128 * k:128 * k + NBLK] for k in (7, 8)]
        s_prefix, s_add, s_m1 = (pool2[:, 1152 + k:1153 + k].bitcast(i32) for k in range(3))
        s_count = pool2[:, 1160:1161]
        sel_idx = pool2[:, 1168:1168 + NSEL].bitcast(i32)
        s_digit = pool2[:, 1280:1281 + CAND].bitcast(i32)
        s_cand, s_m, s_f = (pool2[:, 1312 + 32 * k:1312 + 32 * k + CAND].bitcast(i32) for k in range(3))
        s_step, s_counts, s_got = (pool2[:, 1408 + 32 * k:1408 + 32 * k + CAND] for k in range(3))
        s_junks = part(pool2, 18432, (CAND, NBLK))
        s_oh = [part(pool2, 15360 + 512 * k, (512,)).bitcast(f16)[:, 0:BPB * P].rearrange("p (b m) -> p b m", b=BPB)
                for k in range(2)]
        s_pc = [part(pool2, 16384 + 512 * k, (512,)).bitcast(f16)[:, 0:2 * BPB * NSEL].rearrange("p (b m) -> p b m", b=BPB)
                for k in range(2)]
        s_is = [part(pool2, 17408 + 512 * k, (BPB, NSEL)) for k in range(2)]
        fstg = [pool2[:, 1760 + 2 * k:1762 + 2 * k].bitcast(i32) for k in range(FSLOTS)]
        frow = [part(pool2, 2048 + 1024 * k, (2, 2 * D)) for k in range(FSLOTS)]
        f_xh = [part(pool2r, 5120 + 512 * k, (2, SB)) for k in range(FSLOTS)]
        f_xl = [part(pool2r, 14848 + 512 * k, (2, SB)) for k in range(FSLOTS)]
        fo = [part(pool2, 6656 + 512 * k, (2, D)) for k in range(FSLOTS)]
        fh = part(pool2, 8192, (HF // P, SB))
        f_junk = part(pool2, 10240, (2, D))
        fw1_s = part(pool2, 10752, (2, HF))
        fw2_s = part(pool2, 10752 + 2 * HF, (HF // P, D))
        fh_h = part(pool2r, 16384, (HF // P, SB))
        fw1_h = part(pool2r, 20480, (2, HF))
        fw2_h = part(pool2r, 20480 + 2 * HF, (HF // P, D))
        fh_l = part(pool2r, 8192, (HF // P, SB))
        fw1_l = part(pool2r, 10752, (2, HF))
        fw2_l = part(pool2r, 10752 + 2 * HF, (HF // P, D))

        def seg_values(eng, etype, g0, n, prev):
            a = 2 * g0 - (1 if prev else 0)
            k = 2 * n + (1 if prev else 0)
            ap = bnd[0:1, a:a + k] if isinstance(g0, int) else bnd[0:1, ds(a, k)]
            _, v = nc.values_load_multi_w_load_instructions(
                ap, engines=[etype], min_val=0, max_val=NBLK - 1,
                skip_runtime_bounds_check_because="block numbers of node numbers below NPAD")
            v = list(v)
            before = v.pop(0) if prev else None
            return before, [(v[2 * t], v[2 * t + 1]) for t in range(n)]


        def k_place(s, j, t):
            return KG * s + t, j

        def m_place(i, t):
            g = KG * NSUP + t
            return g % RING, g // RING + i

        def bcast(v, n, w=D):
            return v.unsqueeze(1).to_broadcast([P, n, w])

        block = ctx.enter_context(nc.Block())

        @block.sync
        def _(e):
            for a, t in ((0, src), (1, dst)):
                e.dma_start(edges_i[:, a, 0:CH - 1, :],
                            t[0:(CH - 1) * P * GE].rearrange("(c p e) -> p c e", p=P, e=GE)).then_inc(edges_in, 16)
            e.wait_ge(edges_pad, 2)
            o = (CH - 1) * P * GE
            for a, t in ((0, src), (1, dst)):
                e.dma_start(edges_i[0:LASTC, a, CH - 1, :],
                            t[o:FULLG * GE].rearrange("(p e) -> p e", e=GE)).then_inc(edges_in, 16)
                e.dma_start(edges_i[LASTC:LASTC + 1, a, CH - 1, 0:RESTE],
                            t[FULLG * GE:E].rearrange("(p e) -> p e", p=1)).then_inc(edges_in, 16)

            def ln_load(m, s):
                e.dma_start(ln_x[s], rows(x, m * BPB, BPB)).then_inc(ln_x_in[s], 16)
            ln_load(0, 0)
            ln_load(1, 1)

            def ln_io(m, s, j):
                if not (isinstance(m, int) and m >= NBATCH - 2):
                    if past(m, 2):
                        e.wait_ge(ln_lo, m - 1)
                    ln_load(m + 2, (s + 2) % 4)
                if past(m, 1):
                    e.wait_ge(ln_lo, m)
                    e.dma_start(rows(xtab, (m - 1) * BPB, BPB), ln_t[(s + 1) % 2]).then_inc(ln_out[(s + 1) % 2], 16)
            steps(e, ln_io, NBATCH, 4)
            e.wait_ge(ln_lo, NBATCH)
            e.dma_start(rows(xtab, (NBATCH - 1) * BPB, BPB), ln_t[(NBATCH - 1) % 2]).then_inc(ln_out[(NBATCH - 1) % 2], 16)

            e.wait_ge(bnd_ready, 1)
            e.dma_start(bounds_d.rearrange("(c p) k -> p c k", p=P),
                        small_i[:, 0:2 * CH].rearrange("p (c k) -> p c k", k=2)).then_inc(bnd_out, 16)
            e.wait_ge(bnd_out, 16)
            e.dma_start(bnd[0:1, :], bounds_d[0:NG, :].rearrange("(o g) k -> o (g k)", o=1)).then_inc(bnd_in, 16)

            e.wait_ge(ln_out[0], 16 * (NBATCH // 2))
            e.wait_ge(ln_out[1], 16 * (NBATCH // 2))
            for i in range(2):
                e.dma_start(kx[i], rows(x, 2 * i)).then_inc(k_x_in[i], 16)

            def k_io(i, s, j):
                if not (isinstance(i, int) and i >= NSUP - 2):
                    if past(i, 1):
                        e.wait_ge(k_xn, i)
                    e.dma_start(kx[(s + 2) % 3], rows(x, 2 * i + 4)).then_inc(k_x_in[(s + 2) % 3], 16)
                e.wait_ge(k_xnT, i + 1)
                e.dma_start(turned(xt_d, i), flat(kxT[s])).then_inc(xt_out[s], 16)
                e.wait_ge(k_Q, i + 1)
                e.dma_start(turned(q_d, i), flat(qout[s])).then_inc(q_out[s], 16)
            steps(e, k_io, NSUP, 3, 2)
            for s in range(3):
                e.wait_ge(q_out[s], 16 * len(range(s, NSUP, 3)))
                e.wait_ge(xt_out[s], 16 * len(range(s, NSUP, 3)))
            e.wait_ge(k_acc, NSUP)

            def m_load(i, s):
                e.dma_start(mx[s], rows(x, 2 * i)).then_inc(m_x_in[s], 16)
                e.dma_start(flat(mq[s]), turned(q_d, i)).then_inc(m_q_in[s], 16)

            def m_load_xT(i, s):
                e.dma_start(flat(mxT[s]), turned(xt_d, i)).then_inc(m_xT_in[s], 16)
            m_load(0, 0)
            m_load_xT(0, 0)

            def m_io(i, s, j):
                if not (isinstance(i, int) and i == NSUP - 1):
                    if past(i, 1):
                        e.wait_ge(m_xs, i)
                        e.wait_ge(m_nd_ps, i)
                    m_load(i + 1, 1 - s)
                if past(i, 2):
                    e.wait_ge(m_r, i - 1)
                    e.dma_start(rows(r_d, 2 * i - 4), mr[s]).then_inc(r_out[s], 16)
                if not (isinstance(i, int) and i == NSUP - 1):
                    if past(i, 1):
                        e.wait_ge(m_h1_ps, 2 * i)
                    m_load_xT(i + 1, 1 - s)
            steps(e, m_io, NSUP, 2)
            for i in (NSUP - 2, NSUP - 1):
                e.wait_ge(m_r, i + 1)
                e.dma_start(rows(r_d, 2 * i), mr[i % 2]).then_inc(r_out[i % 2], 16)
            for s in range(2):
                e.wait_ge(r_out[s], 16 * len(range(s, NSUP, 2)))

            def g_load(i, s):
                e.dma_start(gxT[s], turned(xt_d, i).rearrange("p (a b) -> p a b", a=2)).then_inc(g_in[s], 16)
                e.dma_start(gr[s], rows(r_d, 2 * i)).then_inc(g_in[s], 16)
            for i in range(3):
                g_load(i, i)

            def g_store(i, s):
                e.wait_ge(g_base, i + 1)
                e.dma_start(rows(ff_d, 2 * i), gff[s]).then_inc(ff_out[s], 16)
                e.dma_start(rows(out, 2 * i), gff[s][:, :, D:2 * D]).then_inc(ff_out[s], 16)

            def g_io(i, s, j):
                if not (isinstance(i, int) and i >= NSUP - 3):
                    if past(i, 1):
                        e.wait_ge(g_s, i)
                    g_load(i + 3, (s + 3) % 4)
                if past(i, 1):
                    g_store(i - 1, (s + 1) % 2)
            steps(e, g_io, NSUP, 4, 4)
            g_store(NSUP - 1, (NSUP - 1) % 2)
            e.wait_ge(g_ma, NSUP)
            e.dma_start(fw1_s, w1.rearrange("(k p) n -> p k n", p=P)).then_inc(ffw_in, 16)
            e.dma_start(fw2_s, w2.rearrange("(k p) n -> p k n", p=P)).then_inc(ffw_in, 16)
            for s in range(2):
                e.wait_ge(ff_out[s], 32 * len(range(s, NSUP, 2)))
            for s in range(FSLOTS):
                e.wait_ge(f_out[s], 32 * len(range(s, FSTEPS - 1, FSLOTS)) + (16 if (FSTEPS - 1) % FSLOTS == s else 0))

        @block.gpsimd
        def _(e):
            e.memset(edges_i[:, 0, CH - 1, :], 0).then_inc(edges_pad, 1)
            e.memset(edges_i[:, 1, CH - 1, :], PADNODE).then_inc(edges_pad, 1)
            e.memset(ones[:, :], 1.0).then_inc(cst, 1)
            e.memset(ident[:, :], 0.0).then_inc(cst, 1)
            e.wait_ge(cst, 2)
            e.affine_select(out=ident[:, :], in_=ident[:, :], compare_op=ALU.not_equal, fill=1.0,
                            base=0, pattern=[[-1, P]], channel_multiplier=1).then_inc(cst, 1)
            e.affine_select(out=tri[:, :], in_=ones[:, :], compare_op=ALU.is_gt, fill=0.0,
                            base=0, pattern=[[1, P]], channel_multiplier=-1).then_inc(cst, 1)
            hm = headm[:, :].rearrange("p (h d) -> p h d", d=DH)
            e.affine_select(out=hm, in_=ones[:, :].rearrange("p (h d) -> p h d", d=DH), compare_op=ALU.is_ge, fill=0.0,
                            base=0, pattern=[[-DH, P // DH], [0, DH]], channel_multiplier=1).then_inc(cst, 1)
            e.wait_ge(cst, 5)
            e.affine_select(out=hm, in_=hm, compare_op=ALU.is_ge, fill=0.0,
                            base=DH - 1, pattern=[[DH, P // DH], [0, DH]], channel_multiplier=-1).then_inc(cst, 1)
            e.affine_select(out=lastvalid[:, :], in_=ones[:, 0:1], compare_op=ALU.is_gt, fill=0.0,
                            base=LASTROWS, pattern=[[0, 1]], channel_multiplier=-1).then_inc(cst, 1)
            e.iota(iota16[:, :], pattern=[[1, P]], base=0, channel_multiplier=0,
                   allow_small_or_imprecise_dtypes=True).then_inc(cst, 1)
            e.iota(iotaf[:, :], pattern=[[1, P]], base=0, channel_multiplier=0,
                   allow_small_or_imprecise_dtypes=True).then_inc(cst, 1)
            e.iota(blkbase[:, :], pattern=[[P, NBLK]], base=0, channel_multiplier=0,
                   allow_small_or_imprecise_dtypes=True).then_inc(cst, 1)
            e.iota(pcol[:, :], pattern=[[0, 1]], base=0, channel_multiplier=1,
                   allow_small_or_imprecise_dtypes=True).then_inc(cst, 1)
            for b in range(0, NBLK, 14):
                e.memset(agg[:, b:b + 14, :], 0.0).then_inc(agg_zero, 1)

            e.wait_ge(tr_ev, 2 * CH)
            e.wait_ge(ln_out[0], 16 * (NBATCH // 2))
            e.wait_ge(ln_out[1], 16 * (NBATCH // 2))
            e.memset(gath[:, :, 2 * D:2 * D + 1], 1.0).then_inc(ones_set, 1)

            def gather(i, h, n):
                c = srcI[:, ds(RING * i, n), :] if not isinstance(i, int) else srcI[:, RING * i:RING * i + n, :]
                e.tensor_copy(stage[:, h, 0:n, :], c).then_inc(stage_set, 1)
                e.wait_ge(stage_set, i + 1)
                alone(e, stood)
                for s in range(n):
                    if past(i, 1):
                        e.wait_ge(grp_used, RING * (i - 1) + s + 1)
                        alone(e, stood)
                    for t in range(TPG):
                        e.indirect_dma_start(
                            out=gath[:, TPG * s + t, 0:2 * D], out_offset=None, in_=xtab[:, :],
                            in_offset=bass.IndirectOffsetOnAxis(ap=stage[:, h, s, t:t + 1], axis=0)
                        ).then_inc(rows_in[s], 16)
            steps(e, lambda i, h, j: gather(i, h, RING), NG // RING, 2)
            gather(NG // RING, NG // RING % 2, NG % RING)

            e.wait_ge(s_idx, 1)
            for s in range(2):
                e.wait_ge(ff_out[s], 32 * len(range(s, NSUP, 2)))

            def f_gather(i, s, n):
                c = sel_idx[:, ds(2 * i, n)] if not isinstance(i, int) else sel_idx[:, 2 * i:2 * i + n]
                e.tensor_copy(fstg[s][:, 0:n], c).then_inc(fstage[s], 1)

            def f_io(i, s, j):
                n = 1 if isinstance(i, int) and i == FSTEPS - 1 else 2
                if past(i, FSLOTS):
                    e.wait_ge(f_out[s], 32 * j)
                    alone(e, stood)
                f_gather(i, s, n)
                e.wait_ge(fstage[s], j + 1)
                alone(e, stood)
                for u in range(n):
                    e.indirect_dma_start(out=frow[s][:, u, :], out_offset=None, in_=ff_d[:, :],
                                         in_offset=bass.IndirectOffsetOnAxis(ap=fstg[s][:, u:u + 1], axis=0)
                                         ).then_inc(f_in[s], 16)
                if past(i, 2):
                    scatter(i - 2, (s + 1) % FSLOTS, 2, P)

            def scatter(i, s, n, r):
                e.wait_ge(f_o, i + 1)
                alone(e, stood)
                for u in range(n):
                    e.indirect_dma_start(out=out[:, :], in_=fo[s][0:r, u, :], in_offset=None,
                                         out_offset=bass.IndirectOffsetOnAxis(ap=fstg[s][0:r, u:u + 1], axis=0)
                                         ).then_inc(f_out[s], 16)
            steps(e, f_io, FSTEPS, FSLOTS, 2)
            scatter(FSTEPS - 2, (FSTEPS - 2) % FSLOTS, 2, P)
            scatter(FSTEPS - 1, (FSTEPS - 1) % FSLOTS, 1, LASTSEL)

        @block.vector
        def _(e):
            v = nc.vector
            own = Chain(e, own_dve)
            pair = e.alloc_register("dve_pair")
            e.reg_mov(pair, 0)

            v.memset(small[:, 40:41], 0.0).then_inc(seg_added, 2)
            v.memset(small[:, 41:42], 0.0).then_inc(seg_done, 2)

            e.wait_ge(edges_in, 96)
            e.wait_ge(edges_pad, 2)
            for a in range(2):
                v.tensor_copy(edges_f[:, a, :, :], edges_i[:, a, :, :]).then_inc(edges_cast, 1)
            e.wait_ge(edges_cast, 2)
            lo_hi = small[:, 48:48 + 2 * CH].rearrange("p (c k) -> p c k", k=2)
            v.tensor_reduce(lo_hi[:, :, 0], edges_f[:, 1, :, :], AX.X, ALU.min).then_inc(own_dve, 1)
            v.tensor_reduce(lo_hi[:, :, 1], edges_f[:, 1, :, :], AX.X, ALU.max).then_inc(own_dve, 1)
            e.wait_ge(own_dve, 2)
            own.at(2)
            own.link(v.tensor_copy(small_i[:, 0:2 * CH], small[:, 48:48 + 2 * CH]))
            v.tensor_scalar(small_i[:, 0:2 * CH], small_i[:, 0:2 * CH], 7, None, ALU.arith_shift_right
                            ).then_inc(bnd_ready, 1)
            for c in range(CH):
                n = min(P, NG - c * P)
                e.wait_ge(tr_ps, CH + c + 1)
                v.tensor_copy(dstF[:, c * P:c * P + n, :],
                              bank((CH + c) % 8, (TPG, P)).rearrange("p t g -> p g t")[:, 0:n, :]).then_inc(tr_ev, 1)
            e.wait_ge(tr_ps, 2 * CH + 2)
            v.tensor_copy(wlT[:, :, :], bank(0)).then_inc(tr_ev, 1)
            v.tensor_copy(wrT[:, :, :], bank(1)).then_inc(tr_ev, 1)

            def cols(t, m):
                return t[:, m * BPB:m * BPB + BPB] if isinstance(m, int) else t[:, ds(m * BPB, BPB)]

            def ln_body(m, s, j):
                own.at(3 + 3 * m)
                e.wait_ge(ln_x_in[s], 16 * j + 16)
                for k in range(BPB):
                    last = v.bn_stats(stats[:, k, :], ln_x[s][:, k, :])
                own.link(last)
                alone(e, stood)
                for k in range(BPB):
                    last = v.bn_aggr(mv[:, k, :], stats[:, k, :])
                own.link(last)
                own.link(v.tensor_scalar(ln_ve, mv[:, :, 1], LN_EPS, None, ALU.add))
                v.reciprocal(ln_rc, ln_ve).then_inc(ln_var, 1)
                e.wait_ge(ln_rstd, m + 1)
                v.scalar_tensor_tensor(out=cols(nmr, m), in0=mv[:, :, 0], scalar=-1.0, in1=cols(rstd, m),
                                       op0=ALU.mult, op1=ALU.mult).then_inc(ln_tab, 1)
                if past(m, 1):
                    ln_low(m - 1, (s + 3) % 4)

            def ln_low(m, s):
                e.wait_ge(ln_hi, m + 1)
                v.tensor_tensor(ln_t[s % 2][:, :, D:2 * D], ln_x[s], ln_t[s % 2][:, :, 0:D], ALU.subtract).then_inc(ln_lo, 1)

            steps(e, ln_body, NBATCH, 4)
            ln_low(NBATCH - 1, (NBATCH - 1) % 4)
            e.wait_ge(ln_tab, NBATCH)
            v.tensor_scalar(res_s[:, :], rstd[:, :], 2.0, 1.0, ALU.mult, ALU.add).then_inc(res_set, 1)
            v.tensor_scalar(res_b[:, :], nmr[:, :], 2.0, None, ALU.mult).then_inc(res_set, 1)
            e.wait_ge(ln_out[0], 16 * (NBATCH // 2))
            e.wait_ge(ln_out[1], 16 * (NBATCH // 2))
            v.memset(vaug[:, :, :, P:P + 1], 1.0).then_inc(k_ones, 1)

            e.wait_ge(cst, 11)
            e.wait_ge(agg_zero, NBLK // 14)
            e.wait_ge(bnd_in, 16)
            e.wait_ge(tr_ev, 2 * CH)

            dsts = dstF[:, :, :].rearrange("p g t -> p (g t)")
            onehots = onehot[:, :, :, :].rearrange("p k t m -> p (k t) m")

            def one_hot(g, b, p):
                e.wait_ge(seg_done, p + 1)
                c = dsts[:, g * TPG:(g + 1) * TPG] if isinstance(g, int) else dsts[:, ds(g * TPG, TPG)]
                shape = [P, TPG, P]
                v.scalar_tensor_tensor(out=onehots[:, ds(p % 2 * TPG, TPG), :],
                                       in0=iota16[:, :].unsqueeze(1).to_broadcast(shape),
                                       scalar=blkbase[:, ds(b, 1)], in1=c.unsqueeze(2).to_broadcast(shape),
                                       op0=ALU.add, op1=ALU.is_equal).then_inc(oh_ready, 1)

            def add_before(b, p):
                e.wait_ge(seg_done, p + 2)
                v.tensor_tensor(agg[:, ds(b, 1), :], agg[:, ds(b, 1), :],
                                ps[:, ds(BG + (p + 1) % 2, 1), 0:AGW], ALU.add).then_inc(seg_added, 1)

            def seg(g, before, first, last):
                p = e.snap(pair)
                one_hot(g, first, p)
                if before is not None:
                    add_before(before, p)
                    e.wait_ge(seg_added, p + 2)
                    e.sem_inc(grp_used, 1)
                e.reg_add(pair, pair, 1)
                with e.If(first < last):
                    with e.Fori(first + 1, last + 1) as b:
                        q = e.snap(pair)
                        one_hot(g, b, q)
                        add_before(b - 1, q)
                        e.reg_add(pair, pair, 1)

            def k_body(i, s, j):
                before, spans = seg_values(e, mybir.EngineType.DVE, KG * i, KG, past(i, 1))
                seg(KG * i, before, *spans[0])
                e.wait_ge(k_kv_ps, i + 1)
                v.tensor_scalar(kmin, bank(BC), 0.0, None, ALU.min).then_inc(k_kmin, 1)
                seg(KG * i + 1, spans[0][1], *spans[1])
                e.wait_ge(k_kexp, i + 1)
                if past(i, 1):
                    e.wait_ge(k_acc, i)
                v.scalar_tensor_tensor(out=kk_s, in0=bank(BC), scalar=0.0, in1=kmin,
                                       op0=ALU.max, op1=ALU.add).then_inc(k_K, 1)
                e.wait_ge(k_q_ps, i + 1)
                v.tensor_scalar(qmin, bank(BB), 0.0, None, ALU.min).then_inc(k_qmin, 1)
                e.wait_ge(k_qexp, i + 1)
                if past(i, 3):
                    e.wait_ge(q_out[s], 16 * j)
                v.scalar_tensor_tensor(out=qout[s], in0=bank(BB), scalar=0.0, in1=qmin,
                                       op0=ALU.max, op1=ALU.add).then_inc(k_Q, 1)
            steps(e, k_body, NSUP, 3)

            e.wait_ge(k_acc, NSUP)
            for c in range(2):
                a = ps[:, BE, c * (P + 1):c * (P + 1) + P]
                v.scalar_tensor_tensor(out=kvbd[:, c, :], in0=a, scalar=1.0 / N, in1=headm[:, :],
                                       op0=ALU.mult, op1=ALU.mult)
                last = v.tensor_copy(small[:, 42 + c:43 + c], ps[:, BE, c * (P + 1) + P:(c + 1) * (P + 1)])
            last.then_inc(kvbd_set, 1)
            e.wait_ge(kvbd_set, 1)
            for c in range(2):
                last = v.tensor_scalar(kshd[:, c, :], headm[:, :].rearrange("p (h d) -> p h d", d=DH)[:, :, 0],
                                       small[:, 42 + c:43 + c], None, ALU.mult)
            last.then_inc(kvbd_set, 1)

            def norm_stats(src, k, var_sem, base):
                own.at(base)
                for u in range(2):
                    last = v.bn_stats(ln_st[k][:, u, :], src[:, u, :])
                own.link(last)
                alone(e, stood)
                for u in range(2):
                    last = v.bn_aggr(ln_mv[k][:, u, :], ln_st[k][:, u, :])
                own.link(last)
                v.tensor_scalar(ln_ng[k], ln_mv[k][:, :, 0], -1.0, None, ALU.mult)
                own.link(v.tensor_scalar(ln_v2[k], ln_mv[k][:, :, 1], LN_EPS, None, ALU.add))
                v.reciprocal(ln_c2[k], ln_v2[k]).then_inc(var_sem, 1)

            own_m = 3 + 3 * NBATCH

            def m_end(i, s, ch):
                e.wait_ge(m_n2, i + 1)
                own.at(ch)
                own.link(v.tensor_tensor(mn2, mn2, bcast(g2_s[:, :], 2), ALU.mult))
                own.link(v.tensor_tensor(mn2, mn2, bcast(b2_s[:, :], 2), ALU.add))
                e.wait_ge(m_xs, i + 1)
                v.tensor_tensor(mr[s], mn2, mr[s], ALU.add).then_inc(m_r, 1)

            def m_body(i, s, j):
                g0 = KG * NSUP + MG * i
                before, spans = seg_values(e, mybir.EngineType.DVE, g0, MG, True)
                ch = own_m + 10 * i - (10 if past(i, 2) else 5 if past(i, 1) else 0)
                seg(g0, before, *spans[0])
                if past(i, 2):
                    e.wait_ge(m_h2_ps, i - 1)
                    norm_stats(bank(BF), 1, m_v2, ch)
                    ch = ch + 3
                e.wait_ge(m_nd_ps, i + 1)
                own.at(ch)
                own.link(v.tensor_scalar(mden[:, :], ps[:, BC, 0:2 * HEADS], ATT_EPS, 1.0 / N, ALU.add, ALU.mult))
                own.link(v.reciprocal(mden[:, :], mden[:, :]))
                heads = (lambda t: t.rearrange("p u (h d) -> p (u h) d", d=DH))
                v.tensor_tensor(heads(mmsg), heads(bank(BB)),
                                mden[:, :].unsqueeze(2).to_broadcast([P, 2 * HEADS, DH]), ALU.mult).then_inc(m_msg, 1)
                seg(g0 + 1, spans[0][1], *spans[1])
                ch = ch + 2
                if past(i, 2):
                    m_end(i - 2, s, ch)
                    ch = ch + 2
                for t in range(2, 4):
                    seg(g0 + t, spans[t - 1][1], *spans[t])
                e.wait_ge(m_y_ps, i + 1)
                norm_stats(bank(BC), 0, m_v1, ch)
                for t in range(4, MG):
                    seg(g0 + t, spans[t - 1][1], *spans[t])
            steps(e, m_body, NSUP, 2)
            ch = own_m + 10 * NSUP - 10
            for i in (NSUP - 2, NSUP - 1):
                e.wait_ge(m_h2_ps, i + 1)
                norm_stats(bank(BF), 1, m_v2, ch)
                m_end(i, i % 2, ch + 3)
                ch = ch + 5

            p = e.snap(pair)
            add_before(NBLK - 1, p)
            e.wait_ge(seg_added, p + 2)
            base = own_m + 10 * NSUP
            own.at(base)
            own.link(v.tensor_scalar(rcnt[:, :], agg[:, :, D], 1.0, None, ALU.max))
            own.link(v.reciprocal(rcnt[:, :], rcnt[:, :]))
            for s in range(2):
                e.wait_ge(r_out[s], 16 * len(range(s, NSUP, 2)))

            own_g = base + 2

            v.memset(small[:, 43:44], 0.0).then_inc(agg_done, 1)

            def g_router(i, s, ch):
                e.wait_ge(g_base, i + 1)
                if past(i, 1):
                    e.wait_ge(g_w, i)
                for u in range(2):
                    last = v.tensor_tensor_reduce(out=gs[:, u, :], in0=gff[s][:, u, 0:D], in1=wr_s[:, :], scale=1.0,
                                                  scalar=0.0, op0=ALU.mult, op1=ALU.add,
                                                  accum_out=small[:, 44 + u:45 + u])
                last.then_inc(own_dve, 1)
                e.wait_ge(own_dve, ch + 1)
                v.tensor_scalar(wtok[:, ds(2 * i, 2)], small[:, 44:46], br_s[:, 0:1], None, ALU.add).then_inc(g_w, 1)

            def g_body(i, s, j):
                ch = own_g + 5 * i - (1 if past(i, 1) else 0)
                s4, s = s, s % 2
                e.wait_ge(g_in[s4], 32 * j + 32)
                e.wait_ge(g_ps, i + 1)
                own.at(ch)
                own.link(v.tensor_tensor(gs, bank(BB + s), bcast(bl_s[:, :], 2), ALU.add))
                if past(i, 2):
                    e.wait_ge(g_base, i - 1)
                v.scalar_tensor_tensor(out=gx1[s], in0=gs, scalar=0.0, in1=gr[s4],
                                       op0=ALU.max, op1=ALU.add).then_inc(g_s, 1)
                e.wait_ge(g_s, i + 1)
                norm_stats(gx1[s], s, g_v, ch + 1)
                if past(i, 1):
                    g_router(i - 1, 1 - s, ch + 4)
            steps(e, g_body, NSUP, 4)
            g_router(NSUP - 1, (NSUP - 1) % 2, own_g + 5 * NSUP - 1)

            own.at(own_g + 5 * NSUP)
            e.wait_ge(g_w, NSUP)
            lastw = wtok[:, NBLK - 1:NBLK]
            own.link(v.tensor_scalar(small[:, 0:1], lastvalid[:, :], 1.0, 3.4e38, ALU.subtract, ALU.mult))
            own.link(v.tensor_tensor(lastw, lastw, lastvalid[:, :], ALU.mult))
            own.link(v.tensor_tensor(lastw, lastw, small[:, 0:1], ALU.add))
            own.link(v.memset(s_prefix, 0))
            own.link(v.tensor_copy(s_digit, iotaf[:, 0:CAND + 1]))
            own.link(v.tensor_scalar(s_digit, s_digit, 32 - DIGIT, None, ALU.logical_shift_left))
            s0 = own_g + 5 * NSUP + own.n

            def floats(f, m, keys):
                own.link(v.tensor_scalar(m, keys, 31, -1, ALU.arith_shift_right, ALU.bitwise_xor))
                own.link(v.tensor_scalar(m, m, -(1 << 31), None, ALU.bitwise_or))
                own.link(v.tensor_tensor(f, m, keys, ALU.bitwise_xor))

            def key_digit(i, s, j):
                own.at(s0 + 9 * i)
                own.link(v.tensor_tensor(s_cand, s_digit[:, 1:CAND + 1], s_prefix.to_broadcast([P, CAND]), ALU.bitwise_or))
                floats(s_f, s_m, s_cand)
                v.tensor_tensor(s_step, s_digit[:, 1:CAND + 1], s_digit[:, 0:CAND], ALU.subtract)
                for k in range(CAND):
                    last = v.tensor_scalar(s_junks[:, k, :], wtok[:, :], s_f[:, k:k + 1].bitcast(f32), None, ALU.is_ge, ALU.add,
                                           accum_out=s_counts[:, k:k + 1])
                last.then_inc(s_cnt, 1)
                e.wait_ge(s_tot, i + 1)
                own.link(v.scalar_tensor_tensor(out=s_got, in0=ps[:, BA, 0:CAND], scalar=float(KK), in1=s_step,
                                                op0=ALU.is_ge, op1=ALU.mult))
                own.link(v.tensor_reduce(s_count, s_got, AX.X, ALU.add))
                own.link(v.tensor_copy(s_add, s_count))
                own.link(v.tensor_tensor(s_prefix, s_prefix, s_add, ALU.bitwise_or))
                own.link(v.tensor_scalar(s_digit, s_digit, DIGIT, None, ALU.logical_shift_right))
            steps(e, key_digit, NDIG, 2)
            own.at(s0 + 9 * NDIG)
            floats(s_f[:, 0:1], s_m1, s_prefix)
            thr = s_f[:, 0:1].bitcast(f32)
            own.link(v.tensor_scalar(s_gt, wtok[:, :], thr, None, ALU.is_gt))
            own.link(v.tensor_reduce(s_count, s_gt, AX.X, ALU.add))
            v.tensor_scalar(s_eq, wtok[:, :], thr, None, ALU.is_equal).then_inc(s_cnt, 1)

            def ranks(n):
                e.wait_ge(s_tot, n)
                own.link(v.memset(s_sum[0][:, 0:1], 0.0))
                own.link(v.tensor_copy(s_sum[0][:, 1:NBLK], ps[:, BC, 0:NBLK - 1]))
                k, a = 1, 0
                while k < NBLK:
                    v.tensor_copy(s_sum[1 - a][:, 0:k], s_sum[a][:, 0:k])
                    own.link(v.tensor_tensor(s_sum[1 - a][:, k:NBLK], s_sum[a][:, k:NBLK],
                                             s_sum[a][:, 0:NBLK - k], ALU.add))
                    k, a = 2 * k, 1 - a
                own.link(v.tensor_tensor(s_rank, s_sum[a][:, 0:NBLK], ps[:, BB, 0:NBLK], ALU.add))

            ranks(NDIG + 1)
            own.link(v.tensor_scalar(small[:, 0:1], ps[:, BA, 0:1], -1.0, float(KK), ALU.mult, ALU.add))
            own.link(v.tensor_scalar(s_rank, s_rank, small[:, 0:1], None, ALU.is_lt))
            own.link(v.tensor_tensor(s_eq, s_eq, s_rank, ALU.mult))
            v.tensor_tensor(s_eq, s_eq, s_gt, ALU.add).then_inc(s_cnt, 1)
            ranks(NDIG + 2)
            own.link(v.tensor_copy(s_pos, s_rank))
            own.link(v.tensor_scalar(s_q, s_pos, 7, None, ALU.arith_shift_right))
            own.link(v.tensor_copy(s_colf, s_q))
            own.link(v.tensor_scalar(s_q, s_pos, P - 1, None, ALU.bitwise_and))
            own.link(v.tensor_copy(s_rank, s_q))
            own.link(v.scalar_tensor_tensor(out=s_rank, in0=s_rank, scalar=1.0, in1=s_eq, op0=ALU.add, op1=ALU.mult))
            own.link(v.tensor_scalar(s_rank, s_rank, 1.0, None, ALU.subtract))

            def place_blocks(c, s, j):
                if past(c, 2):
                    e.wait_ge(s_mm, c - 1)
                b = (lambda t: (t[:, ds(c * BPB, BPB)] if not isinstance(c, int) else t[:, c * BPB:c * BPB + BPB]).unsqueeze(2))
                v.tensor_tensor(s_oh[s], bcast(iotaf[:, :], BPB, P), b(s_rank).to_broadcast([P, BPB, P]), ALU.is_equal)
                v.tensor_tensor(s_is[s], bcast(iotaf[:, 0:NSEL], BPB, NSEL), b(s_colf).to_broadcast([P, BPB, NSEL]),
                                ALU.is_equal).then_inc(own_dve, 1)
                e.wait_ge(own_dve, s_own + 1 + c)
                v.tensor_scalar(s_pc[s][:, :, 0:NSEL], s_is[s], pcol[:, 0:1], None, ALU.mult)
                v.tensor_tensor(s_pc[s][:, :, NSEL:2 * NSEL], s_is[s], b(iotaf).to_broadcast([P, BPB, NSEL]),
                                ALU.mult).then_inc(s_a, 1)
            s_own = own.base + own.n
            steps(e, place_blocks, NBATCH, 2)
            e.wait_ge(s_mm, NBATCH)
            own.at(s_own + NBATCH)
            own.link(v.tensor_scalar(s_sum[0][:, 0:NSEL], ps[:, BD, NSEL:2 * NSEL], float(P), None, ALU.mult))
            v.tensor_tensor(sel_idx, s_sum[0][:, 0:NSEL], ps[:, BD, 0:NSEL], ALU.add).then_inc(s_idx, 1)

            e.wait_ge(f_wh, 2)
            v.tensor_tensor(fw1_l, fw1_s, fw1_h.bitcast(f32), ALU.subtract).then_inc(f_wl, 1)
            v.tensor_tensor(fw2_l, fw2_s, fw2_h.bitcast(f32), ALU.subtract).then_inc(f_wl, 1)

            def f_low_x(i, s):
                e.wait_ge(f_xT_h, i + 1)
                if past(i, FSLOTS):
                    e.wait_ge(f_h_ps, 4 * (i - FSLOTS + 1))
                v.tensor_tensor(f_xl[s], bank(BA), f_xh[s].bitcast(f32), ALU.subtract).then_inc(f_xT, 1)

            f_low_x(0, 0)

            def f_body(i, s, j):
                n = 1 if isinstance(i, int) and i == FSTEPS - 1 else 2
                for h in range(4):
                    e.wait_ge(f_hh, 4 * i + h + 1)
                    c = slice(2 * h, 2 * h + 2)
                    v.tensor_tensor(fh_l[:, c, :], fh[:, c, :], fh_h[:, c, :].bitcast(f32), ALU.subtract).then_inc(f_h, 1)
                if not (isinstance(i, int) and i == FSTEPS - 1):
                    f_low_x(i + 1, (s + 1) % FSLOTS)
                e.wait_ge(f_in[s], 32 * j + 16 * n)
                if past(i, 1):
                    e.wait_ge(f_o, i)
                for u in range(n):
                    last = v.tensor_tensor_reduce(out=f_junk[:, u, :], in0=frow[s][:, u, 0:D], in1=wr_s[:, :], scale=1.0,
                                                  scalar=0.0, op0=ALU.mult, op1=ALU.add,
                                                  accum_out=small[:, 44 + u:45 + u])
                last.then_inc(f_w, 1)
                e.wait_ge(f_w, 2 * i + 1)
                v.tensor_scalar(small[:, 46:46 + n], small[:, 44:44 + n], br_s[:, 0:1], None, ALU.add).then_inc(f_w, 1)
                e.wait_ge(f_y_ps, i + 1)
                v.tensor_tensor(f_junk[:, 0:n, :], bank(BF)[:, 0:n, :], bcast(fb2_s[:, :], n), ALU.add).then_inc(f_yb, 1)
                e.wait_ge(f_yb, i + 1)
                e.wait_ge(f_w, 2 * i + 2)
                if past(i, FSLOTS):
                    e.wait_ge(f_out[s], 32 * j)
                for u in range(n):
                    last = v.scalar_tensor_tensor(out=fo[s][:, u, :], in0=f_junk[:, u, :], scalar=small[:, 46 + u:47 + u],
                                                  in1=frow[s][:, u, D:2 * D], op0=ALU.mult, op1=ALU.add)
                last.then_inc(f_o, 1)
            steps(e, f_body, FSTEPS, FSLOTS, 2)

        @block.scalar
        def _(e):
            a = nc.scalar
            own = Chain(e, own_act)
            e.dma_start(wlr_n[:, 0:2, :], W_l.rearrange("(c p) n -> p c n", p=P)).then_inc(wlr_in, 16)
            e.dma_start(wlr_n[:, 2:4, :], W_r.rearrange("(c p) n -> p c n", p=P)).then_inc(wlr_in, 16)
            loads = [(wq_s[:, :, :], Wq.rearrange("(k p) n -> p k n", p=P)),
                     (wkv_s[:, :, 0:D], Wk.rearrange("(k p) n -> p k n", p=P)),
                     (wkv_s[:, :, D:2 * D], Wv.rearrange("(k p) n -> p k n", p=P)),
                     (wm_s[:, :, :], Wm.rearrange("(k p) n -> p k n", p=P)),
                     (w1_s[:, :, :], W1.rearrange("(k p) n -> p k n", p=P)),
                     (w2_s[:, :, :], W2.rearrange("(k p) n -> p k n", p=P)),
                     (bl_s[:, :], b_l.unsqueeze(0).to_broadcast([P, D])),
                     (g2_s[:, :], g2.unsqueeze(0).to_broadcast([P, D])),
                     (b2_s[:, :], b2.unsqueeze(0).to_broadcast([P, D])),
                     (fb2_s[:, :], fb2.unsqueeze(0).to_broadcast([P, D])),
                     (wr_s[:, :], wr.rearrange("d o -> o d").to_broadcast([P, D])),
                     (br_s[:, :], br.unsqueeze(0).to_broadcast([P, 1])),
                     (g1_s[:, :], g1.rearrange("(c p) -> p c", p=P)),
                     (b1_s[:, :], b1.rearrange("(c p) -> p c", p=P)),
                     (fb1_s[:, :], fb1.rearrange("(c p) -> p c", p=P))]
            with nc.allow_non_contiguous_dma("a few hundred biases"):
                for to, of in loads:
                    e.dma_start(to, of).then_inc(wts_in, 16)

            for c in range(CH):
                n = min(P, NG - c * P)
                e.wait_ge(tr_ps, c + 1)
                a.activation(srcI[:, c * P:c * P + n, :],
                             bank(c % 8, (TPG, P)).rearrange("p t g -> p g t")[:, 0:n, :], ACT.Copy).then_inc(tr_ev, 1)

            e.wait_ge(edges_cast, 2)
            e.wait_ge(tr_ps, 2 * CH + 2)

            def ln_norm(m, s, j):
                c = (lambda k: ds(m * BPB + k, 1) if not isinstance(m, int) else slice(m * BPB + k, m * BPB + k + 1))
                e.wait_ge(ln_var, m + 1)
                a.activation(rstd[:, m * BPB:m * BPB + BPB] if isinstance(m, int) else rstd[:, ds(m * BPB, BPB)],
                             ln_rc, ACT.Sqrt).then_inc(ln_rstd, 1)
                e.wait_ge(ln_tab, m + 1)
                for k in range(BPB):
                    last = a.activation(ln_x[s][:, k, :], ln_x[s][:, k, :], ACT.Identity, bias=nmr[:, c(k)], scale=rstd[:, c(k)])
                last.then_inc(ln_xn, 1)
                e.wait_ge(ln_xn, m + 1)
                if past(m, 2):
                    e.wait_ge(ln_out[s % 2], 16 * (2 * j + s // 2))
                a.activation(ln_t[s % 2][:, :, 0:D], ln_x[s], ACT.Copy).then_inc(ln_hi, 1)
            steps(e, ln_norm, NBATCH, 4)

            def xn_of(to, of, i, done):
                for u in range(2):
                    k = 2 * i + u
                    c = slice(k, k + 1) if isinstance(k, int) else ds(k, 1)
                    last = a.activation(to[:, u, :], of[:, u, :], ACT.Identity, bias=nmr[:, c], scale=rstd[:, c])
                last.then_inc(done, 1)

            e.wait_ge(ln_tab, NBATCH)
            e.wait_ge(k_x_in[0], 16)
            xn_of(kxn, kx[0], 0, k_xn)
            e.wait_ge(k_xT_ps, 1)
            a.activation(kxT[0], bank(BA), ACT.Copy).then_inc(k_xnT, 1)

            def k_body(i, s, j):
                more = not (isinstance(i, int) and i == NSUP - 1)
                s1 = (s + 1) % 3
                if more:
                    e.wait_ge(k_x_in[s1], 16 * (j + (s + 1) // 3) + 16)
                    e.wait_ge(k_xT_ps, i + 1)
                    xn_of(kxn, kx[s1], i + 1, k_xn)
                e.wait_ge(k_kmin, i + 1)
                a.activation(kmin, kmin, ACT.Exp).then_inc(k_kexp, 1)
                if past(i, 1):
                    e.wait_ge(k_acc, i)
                e.wait_ge(k_ones, 1)
                for u in range(2):
                    last = a.activation(vaug[:, u, :, 0:P], bank(BD)[:, u, :].rearrange("p (c n) -> p c n", c=2),
                                        ACT.Copy)
                if not more:
                    for c in range(2):
                        last = a.activation(vaug[:, 1, c, P:P + 1], lastvalid[:, :], ACT.Copy)
                last.then_inc(k_v, 1)
                if more:
                    e.wait_ge(k_xT_ps, i + 2)
                    if past(i, 2):
                        e.wait_ge(k_q_ps, i - 1)
                        e.wait_ge(xt_out[s1], 16 * (j + (s + 1) // 3))
                    a.activation(kxT[s1], bank(BA), ACT.Copy).then_inc(k_xnT, 1)
                e.wait_ge(k_qmin, i + 1)
                a.activation(qmin, qmin, ACT.Exp).then_inc(k_qexp, 1)
            steps(e, k_body, NSUP, 3)

            def m_relu(i):
                for h in range(2):
                    e.wait_ge(m_h1_ps, 2 * i + h + 1)
                    if past(i, 1):
                        e.wait_ge(m_h2_ps, i)
                    a.activation(mh1[:, 2 * h:2 * h + 2, :], bank(BD + h), ACT.Relu).then_inc(m_h1, 1)

            def m_normed(to, of, k, base, done):
                own.at(base)
                own.link(a.activation(ln_f2[k], ln_c2[k], ACT.Sqrt))
                for u in range(2):
                    last = a.activation(ln_b2[k][:, u:u + 1], ln_ng[k][:, u:u + 1], ACT.Copy,
                                        scale=ln_f2[k][:, u:u + 1])
                own.link(last)
                for u in range(2):
                    last = a.activation(to[:, u, :], of[:, u, :], ACT.Identity,
                                        bias=ln_b2[k][:, u:u + 1], scale=ln_f2[k][:, u:u + 1])
                last.then_inc(done, 1)

            def m_norm2(i, base):
                e.wait_ge(m_v2, i + 1)
                if past(i, 1):
                    e.wait_ge(m_r, i)
                m_normed(mn2, bank(BF), 1, base, m_n2)

            def m_body(i, s, j):
                if past(i, 2):
                    m_norm2(i - 2, 4 * i - 4)
                if past(i, 1):
                    m_relu(i - 1)
                e.wait_ge(m_msgT_ps, i + 1)
                a.activation(mmsgT, bank(BB), ACT.Copy).then_inc(m_msgT, 1)
                e.wait_ge(m_v1, i + 1)
                m_normed(myn, bank(BC), 0, 4 * i - (2 if past(i, 1) else 0), m_yn)
                e.wait_ge(m_yT_ps, i + 1)
                for c in range(2):
                    last = a.activation(mynT[:, c, :], bank(BB)[:, c, :], ACT.Identity,
                                        bias=b1_s[:, c:c + 1], scale=g1_s[:, c:c + 1])
                last.then_inc(m_ynT, 1)
                e.wait_ge(m_x_in[s], 16 * j + 16)
                if past(i, 2):
                    e.wait_ge(r_out[s], 16 * j)
                for u in range(2):
                    k = 2 * i + u
                    c = slice(k, k + 1) if isinstance(k, int) else ds(k, 1)
                    last = a.activation(mr[s][:, u, :], mx[s][:, u, :], ACT.Identity, bias=res_b[:, c], scale=res_s[:, c])
                last.then_inc(m_xs, 1)
            steps(e, m_body, NSUP, 2)
            m_norm2(NSUP - 2, 4 * NSUP - 4)
            m_relu(NSUP - 1)
            m_norm2(NSUP - 1, 4 * NSUP - 2)

            def g_means(i, s):
                for u in range(2):
                    c = ds(2 * i + u, 1) if not isinstance(i, int) else slice(2 * i + u, 2 * i + u + 1)
                    last = a.activation(gma[s][:, u, :], agg[:, c, 0:D], ACT.Copy, scale=rcnt[:, c])
                last.then_inc(g_ma, 1)

            def g_turned(i, s):
                e.wait_ge(g_T_ps, i + 1)
                if past(i, 2):
                    e.wait_ge(g_ps, i - 1)
                a.activation(gaT[s], bank(G_T[s]), ACT.Copy).then_inc(g_aT, 1)

            e.wait_ge(agg_done, 1)
            g_means(0, 0)
            g_means(1, 1)
            g_turned(0, 0)
            g_means(2, 0)
            g_turned(1, 1)

            def g_body(i, s, j):
                if not (isinstance(i, int) and i >= NSUP - 2):
                    g_turned(i + 2, s)
                if not (isinstance(i, int) and i >= NSUP - 3):
                    e.wait_ge(g_T_ps, i + 2)
                    g_means(i + 3, 1 - s)
                e.wait_ge(g_v, i + 1)
                own.at(4 * NSUP + 2 * i)
                own.link(a.activation(ln_f2[s], ln_c2[s], ACT.Sqrt))
                for u in range(2):
                    a.activation(ln_b2[s][:, u:u + 1], ln_ng[s][:, u:u + 1], ACT.Copy, scale=ln_f2[s][:, u:u + 1])
                own.link(a.activation(ln_g2[s], ln_f2[s], ACT.Copy, bias=1.0))
                if past(i, 2):
                    e.wait_ge(ff_out[s], 32 * j)
                    e.wait_ge(g_w, i - 1)
                for o_, f in ((0, ln_f2[s]), (D, ln_g2[s])):
                    for u in range(2):
                        last = a.activation(gff[s][:, u, o_:o_ + D], gx1[s][:, u, :], ACT.Identity,
                                            bias=ln_b2[s][:, u:u + 1], scale=f[:, u:u + 1])
                last.then_inc(g_base, 1)
            steps(e, g_body, NSUP, 2, 3)

            e.wait_ge(ffw_in, 32)
            a.activation(fw1_h, fw1_s, ACT.Copy).then_inc(f_wh, 1)
            a.activation(fw2_h, fw2_s, ACT.Copy).then_inc(f_wh, 1)

            def f_copy(i, s):
                e.wait_ge(f_T_ps, i + 1)
                if past(i, FSLOTS):
                    e.wait_ge(f_h_ps, 4 * (i - FSLOTS + 1))
                a.activation(f_xh[s], bank(BA), ACT.Copy).then_inc(f_xT_h, 1)

            f_copy(0, 0)

            def f_high(i, h):
                e.wait_ge(f_g, 4 * i + h + 1)
                a.activation(fh_h[:, 2 * h:2 * h + 2, :], fh[:, 2 * h:2 * h + 2, :], ACT.Copy).then_inc(f_hh, 1)

            def f_body(i, s, j):
                for h in range(4):
                    e.wait_ge(f_h_ps, 4 * i + h + 1)
                    if past(i, 1):
                        e.wait_ge(f_y_ps, i)
                    for c in (2 * h, 2 * h + 1):
                        last = a.activation(fh[:, c, :], bank(BB + h)[:, c % 2, :], ACT.Gelu_apprx_tanh,
                                            bias=fb1_s[:, c:c + 1])
                    last.then_inc(f_g, 1)
                    f_high(i, h)
                if not (isinstance(i, int) and i == FSTEPS - 1):
                    f_copy(i + 1, (s + 1) % FSLOTS)
            steps(e, f_body, FSTEPS, FSLOTS, 2)

        @block.tensor
        def _(e):
            t = nc.tensor
            pair = e.alloc_register("pe_pair")
            e.reg_mov(pair, 0)

            e.wait_ge(cst, 3)
            e.wait_ge(edges_cast, 2)
            for k in range(2 * CH):
                for q in range(TPG):
                    last = t.transpose(bank(k % 8, (TPG, P))[:, q, :], edges_f[:, k // CH, k % CH, q * P:(q + 1) * P],
                                       ident[:, :])
                last.then_inc(tr_ps, 1)
            e.wait_ge(wlr_in, 32)
            e.wait_ge(tr_ev, 2 * CH)
            for k in range(2):
                for i_ in range(2):
                    for o_ in range(2):
                        last = t.transpose(bank(k)[:, i_, o_ * P:(o_ + 1) * P],
                                           wlr_n[:, 2 * k + o_, i_ * P:(i_ + 1) * P], ident[:, :])
                last.then_inc(tr_ps, 1)
            e.wait_ge(wts_in, 16 * 15)
            e.wait_ge(tr_ev, 2 * CH + 2)

            def transposes(b, of):
                for u in range(2):
                    for c in range(2):
                        last = t.transpose(bank(b)[:, c, u * P:(u + 1) * P], of[:, u, c * P:(c + 1) * P], ident[:, :])
                return last

            def seg(slot, use, first, last_b):
                with e.Fori(first, last_b + 1):
                    p = e.snap(pair)
                    e.wait_ge(rows_in[slot], 16 * TPG * use + 16 * TPG)
                    e.wait_ge(oh_ready, p + 1)
                    e.wait_ge(seg_added, p + 1)
                    for q in range(TPG):
                        oh = onehot[:, ds(p % 2, 1), q, :]
                        k = TPG * slot + q
                        t.matmul(ps[:, ds(BG + p % 2, 1), 0:D], oh, gath[:, k, 0:D], start=q == 0, stop=False,
                                 skip_group_check=True)
                        last = t.matmul(ps[:, ds(BG + p % 2, 1), 0:AGW], oh, gath[:, k, D:2 * D + 1], start=False,
                                        stop=q == TPG - 1, skip_group_check=True)
                    last.then_inc(seg_done, 1)
                    e.reg_add(pair, pair, 1)

            e.wait_ge(bnd_in, 16)
            e.wait_ge(ones_set, 1)
            e.wait_ge(agg_zero, NBLK // 14)
            t.matmul(ps[:, BE, 0:2 * (P + 1)], agg[:, 0, 0:P], agg[:, 1:3, 0:P + 1], start=True, stop=False,
                     skip_group_check=True)

            e.wait_ge(k_xn, 1)
            transposes(BA, kxn).then_inc(k_xT_ps, 1)

            def k_sums(i, end):
                e.wait_ge(k_K, i + 1)
                e.wait_ge(k_v, i + 1)
                for u in range(2):
                    for c in range(2):
                        last = t.matmul(ps[:, BE, c * (P + 1):(c + 1) * (P + 1)], kk_s[:, u, c * P:(c + 1) * P],
                                        vaug[:, u, c, :], start=False, stop=end and u == 1 and c == 1,
                                        skip_group_check=True)
                last.then_inc(k_acc, 1)

            def k_body(i, s, j):
                more = not (isinstance(i, int) and i == NSUP - 1)
                e.wait_ge(k_xnT, i + 1)
                if past(i, 1):
                    e.wait_ge(k_K, i)
                    e.wait_ge(k_v, i)
                for u in range(2):
                    for b in range(2):
                        for c in range(2):
                            last = t.matmul(bank(BC + b)[:, u, :], kxT[s][:, c, u * P:(u + 1) * P],
                                            wkv_s[:, c, b * D:(b + 1) * D], start=c == 0, stop=c == 1)
                last.then_inc(k_kv_ps, 1)
                if past(i, 1):
                    k_sums(i - 1, False)
                _, spans = seg_values(e, mybir.EngineType.PE, KG * i, KG, False)
                seg(*k_place(s, j, 0), *spans[0])
                if more:
                    e.wait_ge(k_xn, i + 2)
                    transposes(BA, kxn).then_inc(k_xT_ps, 1)
                if past(i, 1):
                    e.wait_ge(k_Q, i)
                for o_ in range(2):
                    for c in range(2):
                        last = t.matmul(bank(BB)[:, o_, :], wq_s[:, c, o_ * P:(o_ + 1) * P], kxT[s][:, c, :],
                                        start=c == 0, stop=c == 1)
                last.then_inc(k_q_ps, 1)
                seg(*k_place(s, j, 1), *spans[1])
            steps(e, k_body, NSUP, 3)
            k_sums(NSUP - 1, True)

            e.wait_ge(kvbd_set, 2)

            def m_hidden(i, s, j, h):
                if past(i, 1):
                    e.wait_ge(m_h1, 2 * i - 1 + h)
                e.wait_ge(m_xT_in[s], 16 * j + 16)
                for o_ in (2 * h, 2 * h + 1):
                    for c in range(4):
                        last = t.matmul(bank(BD + h)[:, o_ % 2, :], w1_s[:, c, o_ * P:(o_ + 1) * P],
                                        (mxT[s] if c < 2 else mynT)[:, c % 2, :], start=c == 0, stop=c == 3)
                last.then_inc(m_h1_ps, 1)

            def m_mlp_out(i):
                e.wait_ge(m_h1, 2 * i + 2)
                if past(i, 1):
                    e.wait_ge(m_n2, i)
                for u in range(2):
                    for c in range(4):
                        last = t.matmul(bank(BF)[:, u, :], mh1[:, c, u * P:(u + 1) * P], w2_s[:, c, :],
                                        start=c == 0, stop=c == 3)
                last.then_inc(m_h2_ps, 1)

            def m_body(i, s, j):
                e.wait_ge(m_q_in[s], 16 * j + 16)
                if past(i, 1):
                    e.wait_ge(m_ynT, i)
                    e.wait_ge(m_yn, i)
                for u in range(2):
                    for c in range(2):
                        q = mq[s][:, c, u * P:(u + 1) * P]
                        t.matmul(bank(BB)[:, u, c * P:(c + 1) * P], q, kvbd[:, c, :], start=True, stop=True)
                        h = (2 * u + c) * HPC
                        last = t.matmul(ps[:, BC, h:h + HPC], q, kshd[:, c, :], start=True, stop=True)
                last.then_inc(m_nd_ps, 1)
                g0 = KG * NSUP + MG * i
                _, spans = seg_values(e, mybir.EngineType.PE, g0, 1, False)
                seg(*m_place(i, 0), *spans[0])
                if past(i, 1):
                    m_hidden(i - 1, 1 - s, j - 1 + s, 0)
                spans += seg_values(e, mybir.EngineType.PE, g0 + 1, MG - 1, False)[1]
                seg(*m_place(i, 1), *spans[1])
                if past(i, 1):
                    m_hidden(i - 1, 1 - s, j - 1 + s, 1)
                e.wait_ge(m_msg, i + 1)
                transposes(BB, mmsg).then_inc(m_msgT_ps, 1)
                seg(*m_place(i, 2), *spans[2])
                e.wait_ge(m_msgT, i + 1)
                for u in range(2):
                    for c in range(2):
                        last = t.matmul(bank(BC)[:, u, :], mmsgT[:, c, u * P:(u + 1) * P], wm_s[:, c, :],
                                        start=c == 0, stop=c == 1)
                last.then_inc(m_y_ps, 1)
                seg(*m_place(i, 3), *spans[3])
                if past(i, 1):
                    m_mlp_out(i - 1)
                seg(*m_place(i, 4), *spans[4])
                e.wait_ge(m_yn, i + 1)
                transposes(BB, myn).then_inc(m_yT_ps, 1)
                seg(*m_place(i, 5), *spans[5])
            steps(e, m_body, NSUP, 2)
            e.wait_ge(m_ynT, NSUP)
            for h in range(2):
                m_hidden(NSUP - 1, (NSUP - 1) % 2, (NSUP - 1) // 2, h)
            m_mlp_out(NSUP - 1)

            def g_turn(i, s):
                e.wait_ge(g_ma, i + 1)
                if past(i, 2):
                    e.wait_ge(g_aT, i - 1)
                transposes(G_T[s], gma[s]).then_inc(g_T_ps, 1)

            def g_linear(i, s4, j):
                s = s4 % 2
                e.wait_ge(g_in[s4], 32 * j + 32)
                if past(i, 2):
                    e.wait_ge(g_s, i - 1)
                for u in range(2):
                    for of, w in ((gxT[s4], wrT), (gaT[s], wlT)):
                        if w is wlT and u == 0:
                            e.wait_ge(g_aT, i + 1)
                        for c in range(2):
                            last = t.matmul(bank(BB + s)[:, u, :], of[:, c, u * P:(u + 1) * P], w[:, c, :],
                                            start=w is wrT and c == 0, stop=w is wlT and c == 1)
                last.then_inc(g_ps, 1)
            g_turn(0, 0)
            g_turn(1, 1)
            g_linear(0, 0, 0)

            def g_body(i, s, j):
                if not (isinstance(i, int) and i >= NSUP - 2):
                    g_turn(i + 2, s % 2)
                g_linear(i + 1, (s + 1) % 4, j + (s + 1) // 4)
            steps(e, g_body, NSUP - 1, 4, 2)

            def total(i, s, j):
                e.wait_ge(s_cnt, i + 1)
                t.matmul(ps[:, BA, 0:CAND], ones[:, :], s_counts, start=True, stop=True).then_inc(s_tot, 1)
            steps(e, total, NDIG, 2)
            for n in (NDIG, NDIG + 1):
                e.wait_ge(s_cnt, n + 1)
                if n == NDIG:
                    t.matmul(ps[:, BA, 0:1], ones[:, :], s_count, start=True, stop=True)
                t.matmul(ps[:, BB, 0:NBLK], tri[:, :], s_eq, start=True, stop=True)
                t.matmul(ps[:, BC, 0:NBLK], ones[:, :], s_eq, start=True, stop=True).then_inc(s_tot, 1)

            def place_blocks(c, s, j):
                e.wait_ge(s_a, c + 1)
                for k in range(BPB):
                    last = t.matmul(ps[:, BD, 0:2 * NSEL], s_oh[s][:, k, :], s_pc[s][:, k, :],
                                    start=isinstance(c, int) and c == 0 and k == 0,
                                    stop=isinstance(c, int) and c == NBATCH - 1 and k == BPB - 1, skip_group_check=True)
                last.then_inc(s_mm, 1)
            steps(e, place_blocks, NBATCH, 2)

            e.wait_ge(ffw_in, 32)

            def f_T(i, s, j, n):
                e.wait_ge(f_in[s], 32 * j + 16 * n)
                if past(i, 1):
                    e.wait_ge(f_xT, i)
                for u in range(n):
                    for c in range(2):
                        last = t.transpose(bank(BA)[:, c, u * P:(u + 1) * P], frow[s][:, u, c * P:(c + 1) * P],
                                           ident[:, :])
                last.then_inc(f_T_ps, 1)
            f_T(0, 0, 0, 2)

            def split_products(to, left, right, start, stop):
                for k, (l, r) in enumerate(((0, 0), (0, 1), (1, 0))):
                    last = t.matmul(to, left[l], right[r], start=start and k == 0, stop=stop and k == 2)
                return last

            e.wait_ge(f_wl, 2)

            def f_body(i, s, j):
                end = isinstance(i, int) and i == FSTEPS - 1
                n = 1 if end else 2
                e.wait_ge(f_xT, i + 1)
                for o_ in range(HF // P):
                    if past(i, 1) and o_ % 2 == 0:
                        e.wait_ge(f_g, 4 * i - 3 + o_ // 2)
                    for c in range(2):
                        cols = slice(o_ * P, (o_ + 1) * P)
                        last = split_products(bank(BB + o_ // 2)[:, o_ % 2, :],
                                              [w[:, c, cols] for w in (fw1_h, fw1_l)],
                                              [x_[s][:, c, :] for x_ in (f_xh, f_xl)], c == 0, c == 1)
                    if o_ % 2:
                        last.then_inc(f_h_ps, 1)
                if not end:
                    k = 1 if isinstance(i, int) and i == FSTEPS - 2 else 2
                    f_T(i + 1, (s + 1) % FSLOTS, j + (s + 1) // FSLOTS, k)
                if past(i, 1):
                    e.wait_ge(f_yb, i)
                for u in range(n):
                    for c in range(HF // P):
                        if u == 0 and c % 2 == 0:
                            e.wait_ge(f_h, 4 * i + c // 2 + 1)
                        last = split_products(bank(BF)[:, u, :], [h_[:, c, u * P:(u + 1) * P] for h_ in (fh_h, fh_l)],
                                              [w[:, c, :] for w in (fw2_h, fw2_l)], c == 0, c == HF // P - 1)
                last.then_inc(f_y_ps, 1)
            steps(e, f_body, FSTEPS, FSLOTS, 2)


_INS = {"x": "x", "src": "src", "dst": "dst", "W_l": "L0_gnn_W_l", "b_l": "L0_gnn_b_l", "W_r": "L0_gnn_W_r",
        "Wq": "L0_mix_Wq", "Wk": "L0_mix_Wk", "Wv": "L0_mix_Wv", "Wm": "L0_mix_Wm", "W1": "L0_mix_W1",
        "W2": "L0_mix_W2", "g1": "L0_mix_g1", "b1": "L0_mix_b1", "g2": "L0_mix_g2", "b2": "L0_mix_b2",
        "wr": "L0_ffn_wr", "br": "L0_ffn_br", "w1": "L0_ffn_w1", "fb1": "L0_ffn_b1", "w2": "L0_ffn_w2",
        "fb2": "L0_ffn_b2"}


def kernel(**inputs):
    import concourse.bacc as bacc
    from concourse.bass_utils import run_bass_kernel_spmd

    nc = bacc.Bacc("TRN2", target_bir_lowering=False, num_devices=1)
    arrays, args = {}, {}
    for name, key in _INS.items():
        a = np.ascontiguousarray(inputs[key])
        if name == "x":
            padded = np.zeros((NPAD, D), a.dtype)
            padded[:N] = a
            a = padded
        arrays[f"{name}_in"] = a
        args[name] = nc.dram_tensor(f"{name}_in", a.shape, mybir.dt.from_np(a.dtype), kind="ExternalInput").ap()
    args["out"] = nc.dram_tensor("out_rows", (NPAD, D), f32, kind="ExternalOutput").ap()
    build(nc, **args)
    r = run_bass_kernel_spmd(nc, [arrays], core_ids=[0])
    return r.results[0]["out_rows"][:N]
```
